# Optimizing a Trainium2 kernel written in Bass

```python
import numpy as np
import jax
import jax.numpy as jnp

def _softmax(x, axis=-1):
    return jax.nn.softmax(x, axis=axis)

def _gelu(x):
    return jax.nn.gelu(x, approximate=True)

def _silu(x):
    return jax.nn.silu(x)

def _sigmoid(x):
    return jax.nn.sigmoid(x)

def _layernorm(x, axis=-1, eps=1e-05):
    m = jnp.mean(x, axis=axis, keepdims=True)
    v = jnp.var(x, axis=axis, keepdims=True)
    return (x - m) / jnp.sqrt(v + eps)

def _scatter_add(tgt, idx, src, axis=0):
    return tgt.at[idx].add(src)

def _segment_sum(src, seg, n):
    return jax.ops.segment_sum(src, seg, n)
kernel_name = 'mk_decoder_postln_d1_seqx_r4_100193'

def setup_inputs(seed: int=0):
    np.random.seed(seed)
    _w = jnp.asarray

    def _rec_inputs():
        import jax
        import jax.numpy as jnp
        _rk = jax.random.key(seed)
        x = 7.22e-05 + 1 * jax.random.normal(jax.random.fold_in(_rk, 1), (16, 256, 256), jnp.float32)
        _lenS = 256 - jax.random.randint(jax.random.fold_in(_rk, 7), (16,), 0, max(1, 256 // 4) + 1, jnp.int32)
        _lenS2 = 256 - jax.random.randint(jax.random.fold_in(_rk, 8), (16,), 0, max(1, 256 // 4) + 1, jnp.int32)
        _ctx_1024P = jax.random.normal(jax.random.fold_in(_rk, 11), (16, 16, 256), jnp.float32)
        _ctx_1024c = jax.random.dirichlet(jax.random.fold_in(_rk, 511), 0.3 * jnp.ones((16,), jnp.float32), (16, 256))
        _ctx_1024t = jnp.einsum('bsk,bkd->bsd', _ctx_1024c, _ctx_1024P)
        _ctx_1024t = _ctx_1024t * jax.lax.rsqrt(jnp.mean(jnp.square(_ctx_1024t)) + 1e-12) * 0.953939
        ctx_1024 = 4.13588e-05 + 0.999923 * (_ctx_1024t + 0.3 * jax.random.normal(jax.random.fold_in(_rk, 611), (16, 256, 256), jnp.float32))
        _validS = jnp.arange(256)[None, :] < _lenS[:, None]
        _validS2 = jnp.arange(256)[None, :] < _lenS2[:, None]
        _causal = jnp.tril(jnp.ones((256, 256), dtype=bool))
        mask_BxS2_if1 = jnp.where(jnp.ones((16, 256), dtype=bool), 1, 0).astype(jnp.int32)
        return (x, ctx_1024, mask_BxS2_if1)
    x, ctx_1024, mask_BxS2_if1 = _rec_inputs()

    def _L0_attn_setup():
        import jax, jax.numpy as jnp
        import numpy as np
        DIM = 256
        N_HEADS = 16
        HEAD_DIM = DIM // N_HEADS
        B, T = (2, 512)
        ROPE_THETA = 32.0
        EPS = 1e-06

        def precompute_freqs_1d(dim, seq_len, theta):
            freqs = theta ** (-jnp.arange(0, dim, 2, dtype=jnp.float32) / dim)
            t = jnp.arange(seq_len, dtype=jnp.float32)
            ang = t[:, None] * freqs[None, :]
            return (jnp.cos(ang), jnp.sin(ang))

        def _rms_norm(t, w):
            var = jnp.mean(t * t, axis=-1, keepdims=True)
            return t * jax.lax.rsqrt(var + EPS) * w

        def _rope(q, k, cos, sin):
            cos = cos[None, None]
            sin = sin[None, None]
            q1, q2 = jnp.split(q, 2, axis=-1)
            k1, k2 = jnp.split(k, 2, axis=-1)
            q_out = jnp.concatenate([q1 * cos - q2 * sin, q2 * cos + q1 * sin], axis=-1)
            k_out = jnp.concatenate([k1 * cos - k2 * sin, k2 * cos + k1 * sin], axis=-1)
            return (q_out, k_out)
        key = jax.random.key(seed)
        k1, k2, k3, k4, k5 = jax.random.split(key, 5)
        x = jax.random.normal(k1, (B, T, DIM), dtype=jnp.float32)
        w_qkv = jax.random.normal(k2, (3 * DIM, DIM), dtype=jnp.float32) * DIM ** (-0.5)
        w_proj = jax.random.normal(k3, (DIM, DIM), dtype=jnp.float32) * DIM ** (-0.5)
        q_norm_w = 1.0 + 0.1 * jax.random.normal(k4, (HEAD_DIM,), dtype=jnp.float32)
        k_norm_w = 1.0 + 0.1 * jax.random.normal(k5, (HEAD_DIM,), dtype=jnp.float32)
        return {'x': x, 'w_qkv': w_qkv, 'w_proj': w_proj, 'q_norm_w': q_norm_w, 'k_norm_w': k_norm_w}
    _L0_attn_all = _L0_attn_setup()
    _L0_attn_in = {k: v for k, v in _L0_attn_all.items() if k in ('w_qkv', 'w_proj', 'q_norm_w', 'k_norm_w')}
    del _L0_attn_all

    def _L0_xattn_setup():
        import jax, jax.numpy as jnp
        import numpy as np
        D_MODEL = 256
        NUM_HEADS = 16
        D_KEY = D_MODEL // NUM_HEADS
        MASK_FUTURE = True
        NEG_INF = -jnp.inf
        key = jax.random.key(seed)
        ks = jax.random.split(key, 7)
        B, N = (4, 512)
        return {'query': jax.random.normal(ks[0], (B, N, D_MODEL), dtype=jnp.float32), 'key': jax.random.normal(ks[1], (B, N, D_MODEL), dtype=jnp.float32), 'value': jax.random.normal(ks[2], (B, N, D_MODEL), dtype=jnp.float32), 'mask': jnp.ones((B, N), dtype=jnp.int32), 'Wq': jax.random.normal(ks[3], (D_MODEL, D_MODEL), dtype=jnp.float32) * 0.02, 'Wk': jax.random.normal(ks[4], (D_MODEL, D_MODEL), dtype=jnp.float32) * 0.02, 'Wv': jax.random.normal(ks[5], (D_MODEL, D_MODEL), dtype=jnp.float32) * 0.02, 'Wo': jax.random.normal(ks[6], (D_MODEL, D_MODEL), dtype=jnp.float32) * 0.02}
    _L0_xattn_all = _L0_xattn_setup()
    _L0_xattn_in = {k: v for k, v in _L0_xattn_all.items() if k in ('Wq', 'Wk', 'Wv', 'Wo')}
    del _L0_xattn_all

    def _L0_ffn_setup():
        import jax, jax.numpy as jnp
        import numpy as np
        NUM_HEAVY = 256
        N_ITERS = 50
        FETCH_K_RATIO = 9.0 / 8.0
        EPS = 1.0

        def rmsnorm(x, gamma):
            scale = gamma.shape[0] ** 0.5
            normed = x / jnp.maximum(jnp.linalg.norm(x, axis=-1, keepdims=True), 1e-12)
            return normed * scale * gamma

        def feedforward(x, gamma, w1, b1, w2, b2):
            h = rmsnorm(x, gamma)
            h = jax.nn.gelu(h @ w1.T + b1, approximate=False)
            return h @ w2.T + b2

        def coor_descent(s, n_iters, k, eps):
            logk = jnp.log(jnp.asarray(k, s.dtype))
            a0 = jnp.zeros_like(s[..., :1])
            b0 = -s

            def body(carry, _):
                a, b = carry
                a = eps * (logk - jax.nn.logsumexp((s + b) / eps, axis=-1, keepdims=True))
                b = -jax.nn.relu(s + a)
                return ((a, b), None)
            (a, b), _ = jax.lax.scan(body, (a0, b0), None, length=n_iters)
            return jnp.exp((s + a + b) / eps)
        key = jax.random.key(seed)
        ks = jax.random.split(key, 12)
        b, n, dim = (8, 2048, 256)
        d_light, d_heavy = (int(dim * 0.5), dim * 4)

        def lin(k, dout, din):
            bound = 1.0 / np.sqrt(din)
            k1, k2 = jax.random.split(k)
            w = jax.random.uniform(k1, (dout, din), jnp.float32, -bound, bound)
            bb = jax.random.uniform(k2, (dout,), jnp.float32, -bound, bound)
            return (w, bb)
        x = jax.random.normal(ks[0], (b, n, dim), jnp.float32)
        routing_token = jax.random.normal(ks[1], (dim,), jnp.float32)
        w1_l, b1_l = lin(ks[2], d_light, dim)
        w2_l, b2_l = lin(ks[3], dim, d_light)
        w1_h, b1_h = lin(ks[4], d_heavy, dim)
        w2_h, b2_h = lin(ks[5], dim, d_heavy)
        return dict(x=x, routing_token=routing_token, gamma_l=jnp.ones((dim,), jnp.float32), w1_l=w1_l, b1_l=b1_l, w2_l=w2_l, b2_l=b2_l, gamma_h=jnp.ones((dim,), jnp.float32), w1_h=w1_h, b1_h=b1_h, w2_h=w2_h, b2_h=b2_h)
    _L0_ffn_all = _L0_ffn_setup()
    _L0_ffn_in = {k: v for k, v in _L0_ffn_all.items() if k in ('routing_token', 'gamma_l', 'w1_l', 'b1_l', 'w2_l', 'b2_l', 'gamma_h', 'w1_h', 'b1_h', 'w2_h', 'b2_h')}
    del _L0_ffn_all
    return {'x': x, 'ctx_1024': ctx_1024, 'mask_BxS2_if1': mask_BxS2_if1, 'L0_attn_w_qkv': _L0_attn_in['w_qkv'], 'L0_attn_w_proj': _L0_attn_in['w_proj'], 'L0_attn_q_norm_w': _L0_attn_in['q_norm_w'], 'L0_attn_k_norm_w': _L0_attn_in['k_norm_w'], 'L0_xattn_Wq': _L0_xattn_in['Wq'], 'L0_xattn_Wk': _L0_xattn_in['Wk'], 'L0_xattn_Wv': _L0_xattn_in['Wv'], 'L0_xattn_Wo': _L0_xattn_in['Wo'], 'L0_ffn_routing_token': _L0_ffn_in['routing_token'], 'L0_ffn_gamma_l': _L0_ffn_in['gamma_l'], 'L0_ffn_w1_l': _L0_ffn_in['w1_l'], 'L0_ffn_b1_l': _L0_ffn_in['b1_l'], 'L0_ffn_w2_l': _L0_ffn_in['w2_l'], 'L0_ffn_b2_l': _L0_ffn_in['b2_l'], 'L0_ffn_gamma_h': _L0_ffn_in['gamma_h'], 'L0_ffn_w1_h': _L0_ffn_in['w1_h'], 'L0_ffn_b1_h': _L0_ffn_in['b1_h'], 'L0_ffn_w2_h': _L0_ffn_in['w2_h'], 'L0_ffn_b2_h': _L0_ffn_in['b2_h']}

def reference(x, ctx_1024, mask_BxS2_if1, L0_attn_w_qkv, L0_attn_w_proj, L0_attn_q_norm_w, L0_attn_k_norm_w, L0_xattn_Wq, L0_xattn_Wk, L0_xattn_Wv, L0_xattn_Wo, L0_ffn_routing_token, L0_ffn_gamma_l, L0_ffn_w1_l, L0_ffn_b1_l, L0_ffn_w2_l, L0_ffn_b2_l, L0_ffn_gamma_h, L0_ffn_w1_h, L0_ffn_b1_h, L0_ffn_w2_h, L0_ffn_b2_h):
    import jax
    import jax.numpy as jnp

    def _L0_attn_ref(x, w_qkv, w_proj, q_norm_w, k_norm_w):
        import jax, jax.numpy as jnp
        import numpy as np
        DIM = 256
        N_HEADS = 16
        HEAD_DIM = DIM // N_HEADS
        B, T = (2, 512)
        ROPE_THETA = 32.0
        EPS = 1e-06

        def precompute_freqs_1d(dim, seq_len, theta):
            freqs = theta ** (-jnp.arange(0, dim, 2, dtype=jnp.float32) / dim)
            t = jnp.arange(seq_len, dtype=jnp.float32)
            ang = t[:, None] * freqs[None, :]
            return (jnp.cos(ang), jnp.sin(ang))

        def _rms_norm(t, w):
            var = jnp.mean(t * t, axis=-1, keepdims=True)
            return t * jax.lax.rsqrt(var + EPS) * w

        def _rope(q, k, cos, sin):
            cos = cos[None, None]
            sin = sin[None, None]
            q1, q2 = jnp.split(q, 2, axis=-1)
            k1, k2 = jnp.split(k, 2, axis=-1)
            q_out = jnp.concatenate([q1 * cos - q2 * sin, q2 * cos + q1 * sin], axis=-1)
            k_out = jnp.concatenate([k1 * cos - k2 * sin, k2 * cos + k1 * sin], axis=-1)
            return (q_out, k_out)
        Bc, Tc, C = x.shape
        scale = HEAD_DIM ** (-0.5)
        qkv = x @ w_qkv.T
        qkv = qkv.reshape(Bc, Tc, 3, N_HEADS, HEAD_DIM).transpose(2, 0, 3, 1, 4)
        q, k, v = (qkv[0], qkv[1], qkv[2])
        q = _rms_norm(q, q_norm_w)
        k = _rms_norm(k, k_norm_w)
        cos, sin = precompute_freqs_1d(HEAD_DIM, Tc, ROPE_THETA)
        q, k = _rope(q, k, cos, sin)
        attn = jnp.einsum('bhqd,bhkd->bhqk', q, k) * scale
        causal = jnp.triu(jnp.ones((Tc, Tc), dtype=bool), k=1)
        attn = jnp.where(causal, -jnp.inf, attn)
        attn = jax.nn.softmax(attn, axis=-1)
        out = jnp.einsum('bhqk,bhkd->bhqd', attn, v)
        out = out.transpose(0, 2, 1, 3).reshape(Bc, Tc, C)
        return out @ w_proj.T

    def _L0_xattn_ref(query, key, value, mask, Wq, Wk, Wv, Wo):
        import jax, jax.numpy as jnp
        import numpy as np
        D_MODEL = 256
        NUM_HEADS = 16
        D_KEY = D_MODEL // NUM_HEADS
        MASK_FUTURE = True
        NEG_INF = -jnp.inf
        B, Nq, _ = query.shape
        Nk = key.shape[1]

        def proj(x, W, N):
            return (x @ W).reshape(B, N, NUM_HEADS, D_KEY).transpose(0, 2, 1, 3)
        Q = proj(query, Wq, Nq)
        K = proj(key, Wk, Nk)
        V = proj(value, Wv, Nk)
        scores = jnp.einsum('bhqd,bhkd->bhqk', Q, K) / np.sqrt(D_KEY).astype(np.float32)
        scores = jnp.where(mask[:, None, None, :] == 0, NEG_INF, scores)
        if MASK_FUTURE:
            causal = jnp.triu(jnp.ones((Nq, Nk), dtype=jnp.bool_), k=1)
            scores = jnp.where(causal[None, None, :, :], NEG_INF, scores)
        attn = jax.nn.softmax(scores, axis=-1)
        out = jnp.einsum('bhqk,bhkd->bhqd', attn, V)
        out = out.transpose(0, 2, 1, 3).reshape(B, Nq, D_MODEL)
        return out @ Wo

    def _L0_ffn_ref(x, routing_token, gamma_l, w1_l, b1_l, w2_l, b2_l, gamma_h, w1_h, b1_h, w2_h, b2_h):
        import jax, jax.numpy as jnp
        import numpy as np
        NUM_HEAVY = 256
        N_ITERS = 50
        FETCH_K_RATIO = 9.0 / 8.0
        EPS = 1.0

        def rmsnorm(x, gamma):
            scale = gamma.shape[0] ** 0.5
            normed = x / jnp.maximum(jnp.linalg.norm(x, axis=-1, keepdims=True), 1e-12)
            return normed * scale * gamma

        def feedforward(x, gamma, w1, b1, w2, b2):
            h = rmsnorm(x, gamma)
            h = jax.nn.gelu(h @ w1.T + b1, approximate=False)
            return h @ w2.T + b2

        def coor_descent(s, n_iters, k, eps):
            logk = jnp.log(jnp.asarray(k, s.dtype))
            a0 = jnp.zeros_like(s[..., :1])
            b0 = -s

            def body(carry, _):
                a, b = carry
                a = eps * (logk - jax.nn.logsumexp((s + b) / eps, axis=-1, keepdims=True))
                b = -jax.nn.relu(s + a)
                return ((a, b), None)
            (a, b), _ = jax.lax.scan(body, (a0, b0), None, length=n_iters)
            return jnp.exp((s + a + b) / eps)
        b, n, dim = x.shape
        light_out = feedforward(x, gamma_l, w1_l, b1_l, w2_l, b2_l)
        s = jnp.einsum('bnd,d->bn', x, routing_token)
        effective_k = min(NUM_HEAVY * FETCH_K_RATIO, n)
        scores = coor_descent(s, N_ITERS, effective_k, EPS)
        selected_scores, selected_indices = jax.lax.top_k(scores, NUM_HEAVY)
        selected_scores = selected_scores + jax.lax.stop_gradient(1.0 - selected_scores)
        routed = jnp.take_along_axis(x, selected_indices[..., None], axis=1)
        routed_out = feedforward(routed, gamma_h, w1_h, b1_h, w2_h, b2_h)
        routed_out = routed_out * selected_scores[..., None]
        batch_range = jnp.arange(b)[:, None]
        heavy_out = jnp.zeros_like(x).at[batch_range, selected_indices].set(routed_out)
        return light_out + heavy_out
    x = _layernorm(x + _L0_attn_ref(x, L0_attn_w_qkv, L0_attn_w_proj, L0_attn_q_norm_w, L0_attn_k_norm_w), axis=-1)
    x = _layernorm(x + _L0_xattn_ref(x, ctx_1024, ctx_1024, mask_BxS2_if1, L0_xattn_Wq, L0_xattn_Wk, L0_xattn_Wv, L0_xattn_Wo), axis=-1)
    x = _layernorm(x + _L0_ffn_ref(x, L0_ffn_routing_token, L0_ffn_gamma_l, L0_ffn_w1_l, L0_ffn_b1_l, L0_ffn_w2_l, L0_ffn_b2_l, L0_ffn_gamma_h, L0_ffn_w1_h, L0_ffn_b1_h, L0_ffn_w2_h, L0_ffn_b2_h), axis=-1)
    return x

_drawn_inputs = setup_inputs


def setup_inputs(seed=0):
    import zlib

    import numpy as np

    out = dict(_drawn_inputs(seed))
    spreads = {'L0_ffn_gamma_l': (1.0, 0.2), 'L0_ffn_gamma_h': (1.0, 0.2)}
    factors = {'L0_attn_q_norm_w': 2.896,
     'L0_attn_k_norm_w': 3.291,
     'L0_xattn_Wq': 8.0,
     'L0_xattn_Wk': 8.0,
     'L0_ffn_b1_l': 4.873,
     'L0_ffn_b1_h': 4.898,
     'L0_ffn_b2_h': 3.441}
    for name, (base, spread) in spreads.items():
        noise = np.random.default_rng([zlib.crc32(name.encode()), seed]).standard_normal(out[name].shape)
        drawn = base * np.exp(spread * noise) if base else spread * noise
        out[name] = jnp.asarray(drawn.astype(out[name].dtype))
    for name, factor in factors.items():
        out[name] = (out[name] * factor).astype(out[name].dtype)
    return out
```

```python
from contextlib import ExitStack

import numpy as np
import concourse.bass as bass
from concourse import mybir

B, T, D, H = 16, 256, 256, 16
HD = D // H
P = 128
TT = T // P
C = D // P
HC = P // HD
TERMS_Q = (0, 0, 0, 1, 1, 2)
TERMS_K = (0, 1, 2, 0, 1, 0)
NPROD = len(TERMS_Q) * HD
ROW_BIAS = NPROD
ROW_MAX = NPROD + 1
K_MAX = ROW_MAX
K_ALL = ROW_MAX + 3
VW = 32
HG = 4
NG = H // HG
FCH = 9
LIGHT = FCH - 1
BIG = -1e30
NORM_EPS, LN_EPS = 1e-6, 1e-5


def build(nc, io):
    f32, bf16, i32 = mybir.dt.float32, mybir.dt.bfloat16, mybir.dt.int32
    ALU, ACT, AX = mybir.AluOpType, mybir.ActivationFunctionType, mybir.AxisListType
    ctx = ExitStack()
    with ctx:
        def sb(name, shape, dt=f32):
            return ctx.enter_context(nc.sbuf_tensor(name, shape, dt))

        def sem(name):
            return ctx.enter_context(nc.semaphore(name))

        wqk1 = sb("wqk1", [P, C, 2 * D]); wv1 = sb("wv1", [P, C, D]); wo1 = sb("wo1", [P, C, D])
        wq2 = sb("wq2", [P, C, D]); wk2 = sb("wk2", [P, C, D]); wv2 = sb("wv2", [P, C, D])
        wo2 = sb("wo2", [P, C, D])
        w1 = sb("w1", [P, C, FCH * P]); w2 = sb("w2", [P, FCH, D])
        b1 = sb("b1", [P, FCH]); b2 = sb("b2", [P, 2, D]); b2sum = sb("b2sum", [P, D])
        gam = sb("gam", [P, 2, C])
        cs = sb("cs", [P, TT, 2, HD // 2])
        nw = sb("nw", [P, 2, HD])
        ropeC = sb("ropeC", [P, TT, 2, HD]); ropeS = sb("ropeS", [P, TT, 2, HD])
        idf = sb("idf", [P, P]); idb = sb("idb", [P, P], bf16)
        cmask = sb("cmask", [P, 3, P], bf16)
        maski = sb("maski", [B, T], i32); maskf = sb("maskf", [B, T]); maskb = sb("maskb", [B, T], bf16)
        xT = sb("xT", [P, C, T]); ctxT = sb("ctxT", [P, C, T]); x1T = sb("x1T", [P, C, T])
        xnT = sb("xnT", [P, C, T])
        x0 = sb("x0", [P, TT, D])
        y = [None, sb("y1", [P, TT, D]), sb("y2", [P, TT, D]), sb("y3", [P, TT, D])]
        st = [None] + [sb(f"st{a}", [P, TT, 6]) for a in (1, 2, 3)]
        mv = [None] + [sb(f"mv{a}", [P, TT, 2]) for a in (1, 2, 3)]
        rstd = [None] + [sb(f"rstd{a}", [P, TT]) for a in (1, 2, 3)]
        ve = [None] + [sb(f"ve{a}", [P, TT]) for a in (1, 2, 3)]
        xo = [None, sb("x1", [P, TT, D]), sb("x2", [P, TT, D]), sb("x3", [P, TT, D])]
        sq = sb("sq", [P, TT, 2 * D]); ss = sb("ss", [P, TT, 2 * H]); rr = sb("rr", [P, TT, 2 * H]); ms = sb("ms", [P, TT, 2 * H])
        qn = sb("qn", [P, TT, 2 * D]); rot = sb("rot", [P, TT, 2 * D]); qr = sb("qr", [P, TT, 2 * D])
        sq2 = sb("sq2", [P, TT, D]); ss2 = sb("ss2", [P, TT]); xn = sb("xn", [P, TT, D])
        x2b = sb("x2b", [P, TT, D]); rr2 = sb("rr2", [P, TT]); ssm = sb("ssm", [P, TT])
        half_ = sb("half_", [P, TT, 2 * H])
        nat = [None] + [[sb(f"nat{a}{s}", [P, 3, C * T], bf16) for s in "qk"] for a in (1, 2)]
        rest = [None] + [[sb(f"rest{a}{s}", [P, C * T]) for s in "qk"] for a in (1, 2)]
        stk = [None] + [[sb(f"stk{a}{s}", [K_ALL, H, T], bf16) for s in "qk"] for a in (1, 2)]
        va = [None] + [sb(f"va{a}", [P, TT, H, VW]) for a in (1, 2)]
        mx = [None] + [sb(f"mx{a}", [P, H, 3]) for a in (1, 2)]
        nm = [None] + [sb(f"nm{a}", [P, TT, H]) for a in (1, 2)]
        nr = [None] + [sb(f"nr{a}", [P, TT, H]) for a in (1, 2)]
        mp = [None] + [sb(f"mp{a}", [P, TT, 3, H], bf16) for a in (1, 2)]
        mT = [None] + [sb(f"mT{a}", [3 * H, T], bf16) for a in (1, 2)]
        pr = sb("pr", [P, 2 * HG, 3 * P])
        oT = [None] + [sb(f"oT{a}", [P, NG, T]) for a in (1, 2)]
        rden = [None] + [sb(f"rden{a}", [P, TT, H]) for a in (1, 2)]
        on = [None] + [sb(f"on{a}", [P, TT, D]) for a in (1, 2)]
        onT = [None] + [sb(f"onT{a}", [P, C, T]) for a in (1, 2)]
        g = sb("g", [P, FCH, T])
        nd = [None] + [[nc.dram_tensor(f"nd{a}{s}", [3, C, P, T], bf16) for s in "qk"] for a in (1, 2)]
        md = [None] + [nc.dram_tensor(f"md{a}", [3, H * T], bf16) for a in (1, 2)]
        kb = nc.dram_tensor("kb", [B, T], bf16)

        bank = [ctx.enter_context(nc.psum_tensor(f"bank{i}", [P, 512], f32)) for i in range(8)]
        bankb = [bk[:, :].bitcast(bf16) for bk in bank]
        FFN_BANK, OT_BANK = 7, 6

        def two(name):
            return [None, sem(name + "1"), sem(name + "2")]

        s_weights = sem("weights_loaded"); s_const = sem("consts_ready"); s_setup = sem("setup_step")
        s_kb = sem("keybias_stored"); s_pool = sem("pool_step")
        s_xT = sem("xT_loaded"); s_ctxT = sem("ctxT_loaded"); s_x0 = sem("x0_loaded")
        s_qk1 = sem("qk1_ready"); s_sq = sem("squares_ready"); s_ss = sem("dve_ss"); s_rr = sem("rr_ready"); s_ms = sem("meansq_ready")
        s_qn = sem("qn_ready"); s_rot = sem("pool_rot"); s_rope = sem("rope_ready")
        s_v = two("v_ready"); s_va = two("va_ready")
        s_nat = two("nat_ready"); s_hi = two("hi_ready"); s_rest = two("dve_rest"); s_mid = two("dve_mid")
        s_split = two("split_ready"); s_nd = [None] + [[sem(f"nat_stored{a}{s}") for s in "qk"] for a in (1, 2)]; s_stk = two("stack_loaded")
        s_s = two("scores_ready"); s_mx = two("max_ready"); s_nm = two("dve_nm"); s_mp = two("maxparts_ready")
        s_mt = two("maxT_ready"); s_mT = two("maxT_copied"); s_md = two("max_stored"); s_ml = two("max_loaded")
        s_st = two("scoresT_ready"); s_exp = two("exp_ready"); s_prob = two("probs_ready")
        s_pv = two("out_ready"); s_oT = two("outT_copied"); s_ott = two("outtok_ready")
        s_rd = two("dve_rden"); s_on = two("on_ready"); s_ont = two("onT_ready"); s_onT = two("onT_copied")
        s_o = [None, sem("proj1_ready"), sem("proj2_ready"), sem("ffn_ready")]
        s_y = [None] + [sem(f"dve_y{a}") for a in (1, 2, 3)]
        s_bn = [None] + [sem(f"dve_bn{a}") for a in (1, 2, 3)]
        s_mv = [None] + [sem(f"dve_mv{a}") for a in (1, 2, 3)]
        s_rs = [None] + [sem(f"dve_rs{a}") for a in (1, 2, 3)]
        s_ve = [None] + [sem(f"var{a}_ready") for a in (1, 2, 3)]
        s_x = [None] + [sem(f"x{a}_ready") for a in (1, 2, 3)]
        s_x1t = sem("x1T_ready"); s_x1T = sem("x1T_copied")
        s_ss2 = sem("ss2_ready"); s_sc2 = sem("scale2_ready"); s_ssm = sem("ssm_ready"); s_xn = sem("xn_ready")
        s_xnt = sem("xnT_ready"); s_xnT = sem("xnT_copied"); s_x2b = sem("x2b_ready")
        s_h = sem("hidden_ready"); s_g = sem("gelu_ready"); s_out = sem("out_stored")

        def wait(eng, s, value):
            if isinstance(value, int) and value <= 0:
                return
            eng.wait_ge(s, value)

        def wait_apart(eng, *waits):
            waits = [(s, v if isinstance(v, int) else eng.to_reg(v)) for s, v in waits]
            eng.wait_ge(s_const, 1)
            for s, value in waits:
                wait(eng, s, value)

        def iterations(eng, step):
            step(0, True, False, False)
            step(1, True, True, False)
            step(2, True, True, True)
            with eng.Fori(3, B - 1) as i:
                step(i, True, True, True)
            step(B - 1, True, True, True)
            step(B, False, True, True)
            step(B + 1, False, False, True)

        block = ctx.enter_context(nc.Block())

        @block.sync
        def _(sp):
            def load(dst, src, s):
                sp.dma_start(dst, src).then_inc(s, 16)

            load(maski[:, :], io["mask"], s_kb)
            for dst, src in ((wqk1, io["wqk1"]), (wv1, io["wv1"]), (wo1, io["wo1"]), (wq2, io["wq2"]),
                             (wk2, io["wk2"]), (wv2, io["wv2"]), (wo2, io["wo2"]), (w1[:, :, 0:LIGHT * P], io["w1h"]),
                             (w1[:, :, LIGHT * P:FCH * P], io["w1l"]), (w2[:, 0:LIGHT, :], io["w2h"])):
                load(dst[:, :, :] if dst in (wqk1, wv1, wo1, wq2, wk2, wv2, wo2) else dst,
                     src.rearrange("(c p) n -> p c n", p=P), s_weights)
            load(w2[:, LIGHT, :], io["w2l"], s_weights)
            load(b1[:, 0:LIGHT], io["b1h"], s_weights)
            load(b1[:, LIGHT:FCH], io["b1l"], s_weights)
            load(gam[:, :, :], io["gam"], s_weights)
            load(cs[:, :, :, :], io["cossin"].rearrange("(t p) (s d) -> p t s d", p=P, s=2), s_weights)
            load(b2[:, :, :], io["b2"].rearrange("(o s) d -> o s d", o=1).to_broadcast([P, 2, D]), s_weights)
            load(nw[:, :, :], io["nw"].rearrange("(o s) d -> o s d", o=1).to_broadcast([P, 2, HD]), s_weights)
            sp.wait_ge(s_setup, 3)
            load(kb.ap(), maskb[:, :], s_kb)
            sp.wait_ge(s_kb, 32)

            def stacks(a, b):
                for nth, s in enumerate((None, (0, 1), (1, 0))[a]):
                    wait_apart(sp, (s_split[a], 2 * b + nth + 1))
                    wait_apart(sp, (s_stk[a], NSTK[a] * 16 * b))
                    load(nd[a][s].ap().rearrange("p c r t -> r (p c) t"),
                         nat[a][s][:, :, :].rearrange("r p (c t) -> r (p c) t", c=C), s_nd[a][s])
                wait_apart(sp, (s_pv[a], NG * b))
                if a == 2:
                    load(stk[2][1][ROW_BIAS:ROW_BIAS + 1, :, :],
                         kb.ap()[bass.ds(b, 1), :].rearrange("o (h t) -> o h t", h=1).to_broadcast([1, H, T]), s_stk[2])
                for s in range(2):
                    wait_apart(sp, (s_nd[a][s], 16 * (b + 1)))
                    for r, part in enumerate((TERMS_Q, TERMS_K)[s]):
                        load(stk[a][s][r * HD:(r + 1) * HD, :, :],
                             nd[a][s].ap()[part].rearrange("c (j d) t -> d (c j) t", d=HD), s_stk[a])

            def maxima(a, b):
                wait_apart(sp, (s_mT[a], b + 1))
                wait_apart(sp, (s_ml[a], 16 * b))
                load(md[a].ap().rearrange("p (h t) -> (p h) t", h=H), mT[a][:, :], s_md[a])
                wait_apart(sp, (s_md[a], 16 * (b + 1)))
                load(stk[a][0][ROW_MAX:ROW_MAX + 3, :, :], md[a].ap().rearrange("p (h t) -> p h t", h=H), s_ml[a])

            def tokens(dram, b):
                return dram[bass.ds(b, 1)].rearrange("o (t p) d -> p (o t) d", p=P)

            def dims(dram, b):
                return dram[bass.ds(b, 1)].rearrange("o (c p) t -> p (o c) t", p=P)

            NSTK = [0, 2 * len(TERMS_Q), 2 * len(TERMS_Q) + 1]

            def step(i, self_, cross, ffn):
                if self_:
                    wait_apart(sp, (s_y[1], i))
                    load(x0[:, :, :], tokens(io["x"], i), s_x0)
                if cross:
                    stacks(2, i - 1)
                if self_:
                    stacks(1, i)
                    if not isinstance(i, int) or i + 1 < B:
                        wait_apart(sp, (s_v[1], i + 1))
                        load(xT[:, :, :], dims(io["xT"], i + 1), s_xT)
                    wait_apart(sp, (s_v[2], i))
                    load(ctxT[:, :, :], dims(io["ctxT"], i), s_ctxT)
                if cross:
                    maxima(2, i - 1)
                if self_:
                    maxima(1, i)
                if ffn:
                    b = i - 2
                    wait_apart(sp, (s_x[3], TT * (b + 1)))
                    load(tokens(io["out"], b), xo[3][:, :, :], s_out)

            load(xT[:, :, :], dims(io["xT"], 0), s_xT)
            iterations(sp, step)
            sp.wait_ge(s_out, 16 * B)
            for a in (1, 2):
                for s in range(2):
                    sp.wait_ge(s_nd[a][s], 16 * B)
                sp.wait_ge(s_md[a], 16 * B)

        @block.tensor
        def _(pe):
            def mm(out, lhsT, rhs, start, stop, check=False):
                return nc.tensor.matmul(out, lhsT, rhs, start=start, stop=stop, skip_group_check=check)

            def tok_proj(out, src, t, w, lo, n):
                for c in range(C):
                    last = mm(out, src[:, c, t * P:(t + 1) * P], w[:, c, lo:lo + n], c == 0, c == C - 1)
                return last

            def dim_proj(out, w, lo, src):
                for c in range(C):
                    last = mm(out, w[:, c, lo:lo + P], src[:, c, :], c == 0, c == C - 1)
                return last

            def four_transposes(k, src):
                for c in range(C):
                    for t in range(TT):
                        last = nc.tensor.transpose(bank[k][:, c * T + t * P:c * T + (t + 1) * P],
                                                   src[:, t, c * P:(c + 1) * P], idf[:, :])
                return last

            def qkv1(b):
                pe.wait_ge(s_xT, 16 * (b + 1))
                for t in range(TT):
                    wait(pe, (s_onT[1], s_y[1])[t], b)
                    tok_proj(bank[t][:, :], xT, t, wqk1, 0, 2 * D).then_inc(s_qk1, 1)
                wait(pe, s_on[1], TT * b)
                for t in range(TT):
                    last = tok_proj(bank[4][:, t * D:(t + 1) * D], xT, t, wv1, 0, D)
                last.then_inc(s_v[1], 1)

            def transpose_x1(b):
                pe.wait_ge(s_x[1], TT * (b + 1))
                four_transposes(5, xo[1]).then_inc(s_x1t, 1)

            def qkv2(b, self_):
                pe.wait_ge(s_ctxT, 16 * (b + 1))
                for c in range(C):
                    last = dim_proj(bank[3][:, c * T:(c + 1) * T], wk2, c * P, ctxT)
                last.then_inc(s_nat[2], 1)
                if self_:
                    pe.wait_ge(s_va[1], b + 2)
                for t in range(TT):
                    last = tok_proj(bank[4][:, t * D:(t + 1) * D], ctxT, t, wv2, 0, D)
                last.then_inc(s_v[2], 1)
                pe.wait_ge(s_x1T, b + 1)
                for c in range(C):
                    last = dim_proj(bank[2][:, c * T:(c + 1) * T], wq2, c * P, x1T)
                last.then_inc(s_nat[2], 1)

            def transpose_xn(b):
                pe.wait_ge(s_xn, TT * (b + 1))
                four_transposes(5, xn).then_inc(s_xnt, 1)

            def hidden(b, j, cross):
                k = 4 + j % 2
                if j == 0:
                    pe.wait_ge(s_xnT, b + 1)
                    if cross:
                        pe.wait_ge(s_va[2], b + 2)
                elif j >= 2:
                    pe.wait_ge(s_g, FCH * b + j - 1)
                dim_proj(bank[k][:, 0:T], w1, j * P, xnT).then_inc(s_h, 1)

            def transpose_qk1(b, cross):
                pe.wait_ge(s_rope, TT * (b + 1))
                if cross:
                    pe.wait_ge(s_rest[2], 2 * b)
                for s in range(2):
                    four_transposes(2 + s, qr[:, :, s * D:(s + 1) * D]).then_inc(s_nat[1], 1)

            def scores(a, b, h, cross):
                if h == 0:
                    pe.wait_ge(s_stk[a], 16 * (12 if a == 1 else 13) * (b + 1))
                k = h % 2
                if h >= 2:
                    pe.wait_ge(s_mx[a], H * b + h - 1)
                elif a == 1 and cross:
                    pe.wait_ge(s_mx[2], H * b + h - 1)
                q, kk = stk[a]
                mm(bank[k][:, 0:3 * P], idb[:, :], cmask[:, :, :], True, False, True)
                mm(bank[k][:, 0:P], q[0:K_MAX, h, 0:P], kk[0:K_MAX, h, 0:P], False, False, True)
                mm(bank[k][:, P:3 * P], q[0:K_MAX, h, P:T], kk[0:K_MAX, h, :], False, True, True).then_inc(s_s[a], 1)

            def transpose_max(a, b, cross, ffn):
                bank_read = [(s_g, FCH * b)] if a == 2 and ffn else [(s_mT[2], b)] if a == 1 and cross else []
                wait_apart(pe, (s_mp[a], b + 1), *bank_read)
                for t in range(TT):
                    last = nc.tensor.transpose(bankb[5][0:3 * H, t * P:(t + 1) * P], mp[a][:, t, :, :], idb[:, :])
                last.then_inc(s_mt[a], 1)

            def scores_t(a, b, h, cross):
                if h == 0:
                    pe.wait_ge(s_ml[a], 16 * (b + 1))
                k = 2 + h % 2
                if h >= 2:
                    pe.wait_ge(s_exp[a], H * b + h - 1)
                elif a == 1 and cross:
                    pe.wait_ge(s_exp[2], H * b + h - 1)
                q, kk = stk[a]
                mm(bank[k][:, 0:T], kk[0:K_ALL, h, 0:P], q[0:K_ALL, h, :], True, True)
                mm(bank[k][:, T:3 * P], kk[0:K_ALL, h, P:T], q[0:K_ALL, h, P:T], True, True).then_inc(s_st[a], 1)

            def values(a, b, gr):
                pe.wait_ge(s_prob[a], H * b + HG * (gr + 1))
                if gr == 0:
                    pe.wait_ge(s_va[a], b + 1)
                else:
                    pe.wait_ge(s_oT[a], NG * b + gr)
                for key in range(2):
                    for j in range(HG):
                        h = HG * gr + j
                        out = bank[OT_BANK][VW * j:VW * (j + 1), :]
                        if key == 0:
                            mm(out[:, 0:T], va[a][:, 0, h, :], pr[:, h % (2 * HG), 0:T], True, False, True)
                        else:
                            last = mm(out[:, P:T], va[a][:, 1, h, :], pr[:, h % (2 * HG), T:3 * P], False, True, True)
                last.then_inc(s_pv[a], 1)

            def out_tokens(a, b, self_, ffn):
                pe.wait_ge(s_oT[a], NG * (b + 1))
                if a == 2 and ffn:
                    pe.wait_ge(s_g, FCH * b)
                if a == 2 and self_:
                    pe.wait_ge(s_mT[1], b + 2)
                for t in range(TT):
                    for gr in range(NG):
                        last = nc.tensor.transpose(bank[4 + t][:, gr * P:(gr + 1) * P],
                                                   oT[a][:, gr, t * P:(t + 1) * P], idf[:, :])
                    last.then_inc(s_ott[a], 1)

            def out_dims(a, b):
                pe.wait_ge(s_on[a], TT * (b + 1))
                four_transposes(0, on[a]).then_inc(s_ont[a], 1)

            def out_proj(a, b, cross):
                pe.wait_ge(s_onT[a], b + 1)
                if a == 1 and cross:
                    pe.wait_ge(s_y[2], b)
                for t in range(TT):
                    last = tok_proj(bank[1][:, t * D:(t + 1) * D], onT[a], t, (None, wo1, wo2)[a], 0, D)
                last.then_inc(s_o[a], 1)

            def ffn_out(b, t, j):
                if t == 0 and j == 0:
                    wait(pe, s_y[3], b)
                if t == 0:
                    pe.wait_ge(s_g, FCH * b + j + 1)
                last = mm(bank[FFN_BANK][:, t * D:(t + 1) * D], g[:, j, t * P:(t + 1) * P], w2[:, j, :],
                          j == 0, j == FCH - 1)
                if t == TT - 1 and j == FCH - 1:
                    last.then_inc(s_o[3], 1)

            def step(i, self_, cross, ffn):
                if self_:
                    qkv1(i)
                if cross:
                    transpose_x1(i - 1)
                    qkv2(i - 1, self_)
                if ffn:
                    transpose_xn(i - 2)
                    for j in range(FCH):
                        hidden(i - 2, j, cross)
                if self_:
                    transpose_qk1(i, cross)
                for a, b, on_ in ((2, i - 1, cross), (1, i, self_)):
                    if on_:
                        for h in range(H):
                            scores(a, b, h, cross)
                        transpose_max(a, b, cross, ffn)
                shares = [(t, j) for t in range(TT) for j in range(FCH)] if ffn else []
                for a, b, on_ in ((2, i - 1, cross), (1, i, self_)):
                    if on_:
                        for h in range(H):
                            scores_t(a, b, h, cross)
                            if shares and h % 2:
                                ffn_out(i - 2, *shares.pop(0))
                            if h % HG == 1 and h > HG:
                                values(a, b, h // HG - 1)
                        values(a, b, NG - 1)
                        if shares:
                            ffn_out(i - 2, *shares.pop(0))
                        out_tokens(a, b, self_, ffn)
                        out_dims(a, b)
                        out_proj(a, b, cross)
                while shares:
                    ffn_out(i - 2, *shares.pop(0))

            pe.wait_ge(s_weights, 16 * N_WEIGHTS)
            pe.wait_ge(s_const, 1)
            pe.wait_ge(s_setup, N_SETUP)
            iterations(pe, step)

        @block.scalar
        def _(act):
            def copy(out, in_):
                return nc.scalar.activation(out, in_, ACT.Copy)

            def step(i, self_, cross, ffn):
                if self_:
                    b = i
                    for t in range(TT):
                        act.wait_ge(s_qk1, TT * b + t + 1)
                        wait(act, s_ss, TT * b)
                        nc.scalar.activation(sq[:, t, :], bank[t][:, :], ACT.Square).then_inc(s_sq, 1)
                    act.wait_ge(s_v[1], b + 1)
                    wait(act, s_pv[1], NG * b)
                    copy(va[1][:, :, :, 0:HD], bank[4][:, :].rearrange("p (t h d) -> p t h d", t=TT, h=H))\
                        .then_inc(s_va[1], 1)
                if cross:
                    b = i - 1
                    act.wait_ge(s_x1t, b + 1)
                    wait(act, s_nat[2], 2 * b)
                    copy(x1T[:, :, :], bank[5][:, :].rearrange("p (c t) -> p c t", c=C))\
                        .then_inc(s_x1T, 1)
                    high_part(2, b, 1, 0)
                    act.wait_ge(s_v[2], b + 1)
                    wait(act, s_pv[2], NG * b)
                    copy(va[2][:, :, :, 0:HD], bank[4][:, :].rearrange("p (t h d) -> p t h d", t=TT, h=H))\
                        .then_inc(s_va[2], 1)
                    high_part(2, b, 0, 1)
                if ffn:
                    b = i - 2
                    act.wait_ge(s_xnt, b + 1)
                    wait(act, s_h, FCH * b)
                    copy(xnT[:, :, :], bank[5][:, :].rearrange("p (c t) -> p c t", c=C))\
                        .then_inc(s_xnT, 1)
                    for j in range(FCH):
                        act.wait_ge(s_h, FCH * b + j + 1)
                        if j == 0:
                            wait(act, s_o[3], b)
                        nc.scalar.activation(g[:, j, :], bank[4 + j % 2][:, 0:T], ACT.Gelu, bias=b1[:, j:j + 1])\
                            .then_inc(s_g, 1)
                if self_:
                    for s in range(2):
                        high_part(1, i, s, s)
                for a, b, on_ in ((2, i - 1, cross), (1, i, self_)):
                    if on_:
                        for h in range(H):
                            act.wait_ge(s_st[a], H * b + h + 1)
                            slot = h % (2 * HG)
                            if h >= 2 * HG:
                                act.wait_ge(s_pv[a], NG * b + h // HG - 1)
                            else:
                                wait(act, s_pv[3 - a], NG * i - 1 + h // HG)
                            nc.scalar.activation(pr[:, slot, :], bank[2 + h % 2][:, 0:3 * P], ACT.Exp, scale=HD ** -0.5)\
                                .then_inc(s_exp[a], 1)
                            if a == 1 and cross and h == HG + 1:
                                norms(i - 1)
                        act.wait_ge(s_ont[a], b + 1)
                        copy(onT[a][:, :, :], bank[0][:, :].rearrange("p (c t) -> p c t", c=C))\
                            .then_inc(s_onT[a], 1)
                        if a == 2 and not self_:
                            norms(b)

            def norms(b):
                wait(act, s_ssm, b)
                for t in range(TT):
                    act.wait_ge(s_x[2], TT * b + t + 1)
                    nc.scalar.activation(sq2[:, t, :], xo[2][:, t, :], ACT.Square,
                                         accum_out=ss2[:, t:t + 1]).then_inc(s_ss2, 1)

            def high_part(a, b, s, nth):
                act.wait_ge(s_nat[a], 2 * b + nth + 1)
                wait(act, s_nd[a][s], 16 * b)
                copy(nat[a][s][:, 0, :], bank[2 + s][:, :]).then_inc(s_hi[a], 1)

            act.wait_ge(s_weights, 16 * N_WEIGHTS)
            iterations(act, step)

        @block.vector
        def _(dve):
            V = nc.vector

            def split(a, b, s, nth):
                dve.wait_ge(s_hi[a], 2 * b + nth + 1)
                n = nat[a][s]
                V.tensor_tensor(rest[a][s][:, :], bank[2 + s][:, :], n[:, 0, :], ALU.subtract)\
                    .then_inc(s_rest[a], 1)
                dve.wait_ge(s_rest[a], 2 * b + nth + 1)
                V.tensor_copy(n[:, 1, :], rest[a][s][:, :]).then_inc(s_mid[a], 1)
                dve.wait_ge(s_mid[a], 2 * b + nth + 1)
                V.tensor_tensor(n[:, 2, :], rest[a][s][:, :], n[:, 1, :], ALU.subtract).then_inc(s_split[a], 1)

            def maxima(a, b):
                for h in range(H):
                    dve.wait_ge(s_s[a], H * b + h + 1)
                    V.tensor_reduce(mx[a][:, h, :], bank[h % 2][:, 0:3 * P].rearrange("p (k t) -> p k t", k=3),
                                    AX.X, ALU.max, negate=True).then_inc(s_mx[a], 1)
                dve.wait_ge(s_mx[a], H * (b + 1))
                V.tensor_copy(nm[a][:, 0, :], mx[a][:, :, 0])
                V.tensor_tensor(nm[a][:, 1, :], mx[a][:, :, 1], mx[a][:, :, 2], ALU.min).then_inc(s_nm[a], 1)
                dve.wait_ge(s_nm[a], 4 * b + 1)
                wait(dve, s_mt[a], b)
                V.tensor_copy(mp[a][:, :, 0, :], nm[a][:, :, :]).then_inc(s_nm[a], 1)
                dve.wait_ge(s_nm[a], 4 * b + 2)
                V.tensor_tensor(nr[a][:, :, :], nm[a][:, :, :], mp[a][:, :, 0, :], ALU.subtract).then_inc(s_nm[a], 1)
                dve.wait_ge(s_nm[a], 4 * b + 3)
                V.tensor_copy(mp[a][:, :, 1, :], nr[a][:, :, :]).then_inc(s_nm[a], 1)
                dve.wait_ge(s_nm[a], 4 * b + 4)
                V.tensor_tensor(mp[a][:, :, 2, :], nr[a][:, :, :], mp[a][:, :, 1, :], ALU.subtract).then_inc(s_mp[a], 1)

            def max_t(a, b):
                dve.wait_ge(s_mt[a], b + 1)
                wait(dve, s_md[a], 16 * b)
                V.tensor_copy(mT[a][:, :], bankb[5][0:3 * H, 0:T]).then_inc(s_mT[a], 1)

            def out_t(a, b, gr):
                dve.wait_ge(s_pv[a], NG * b + gr + 1)
                wait(dve, s_ott[a], TT * b)
                V.tensor_copy(oT[a][:, gr, :], bank[OT_BANK][:, 0:T]).then_inc(s_oT[a], 1)

            def normalise_heads(a, b):
                for t in range(TT):
                    dve.wait_ge(s_ott[a], TT * b + t + 1)
                    o = bank[4 + t][:, :].rearrange("p (h w) -> p h w", w=VW)
                    V.reciprocal(rden[a][:, t, :], o[:, :, HD]).then_inc(s_rd[a], 1)
                    dve.wait_ge(s_rd[a], TT * b + t + 1)
                    wait(dve, s_ont[a], b)
                    V.tensor_tensor(on[a][:, t, :].rearrange("p (h d) -> p h d", d=HD), o[:, :, 0:HD],
                                    rden[a][:, t, :].rearrange("p (h o) -> p h o", o=1).to_broadcast([P, H, HD]),
                                    ALU.mult).then_inc(s_on[a], 1)

            def layer_norm(a, b, k, resid):
                dve.wait_ge(s_o[a], b + 1)
                wait(dve, s_x[a], TT * b)
                V.tensor_tensor(y[a][:, :, :], bank[k][:, :].rearrange("p (t d) -> p t d", t=TT), resid[:, :, :], ALU.add)\
                    .then_inc(s_y[a], 1)
                dve.wait_ge(s_y[a], b + 1)
                for t in range(TT):
                    V.bn_stats(st[a][:, t, :], y[a][:, t, :]).then_inc(s_bn[a], 1)
                for t in range(TT):
                    wait_apart(dve, (s_bn[a], TT * b + t + 1))
                    V.bn_aggr(mv[a][:, t, :], st[a][:, t, :]).then_inc(s_mv[a], 1)
                dve.wait_ge(s_mv[a], TT * (b + 1))
                wait(dve, s_rs[a], b)
                V.tensor_scalar(ve[a][:, :], mv[a][:, :, 1], LN_EPS, None, ALU.add).then_inc(s_ve[a], 1)
                dve.wait_ge(s_rs[a], b + 1)
                if a == 1:
                    wait(dve, s_x1t, b)
                elif a == 2:
                    wait(dve, s_x2b, b)
                else:
                    wait(dve, s_out, 16 * b)
                for t in range(TT):
                    V.tensor_scalar(xo[a][:, t, :], y[a][:, t, :], mv[a][:, t, 0:1], rstd[a][:, t:t + 1],
                                    ALU.subtract, ALU.mult).then_inc(s_x[a], 1)

            def scale2(b):
                dve.wait_ge(s_ss2, TT * (b + 1))
                wait(dve, s_sc2, b)
                V.tensor_scalar(ssm[:, :], ss2[:, :], 1e-24, None, ALU.max).then_inc(s_ssm, 1)
                dve.wait_ge(s_sc2, b + 1)
                wait(dve, s_xnt, b)
                for t in range(TT):
                    V.tensor_scalar(xn[:, t, :], xo[2][:, t, :], rr2[:, t:t + 1], None, ALU.mult).then_inc(s_xn, 1)

            def step(i, self_, cross, ffn):
                if self_:
                    b = i
                    for t in range(TT):
                        dve.wait_ge(s_sq, TT * b + t + 1)
                        V.tensor_reduce(ss[:, t, :], sq[:, t, :].rearrange("p (h d) -> p h d", d=HD), AX.X, ALU.add)\
                            .then_inc(s_ss, 1)
                    dve.wait_ge(s_ss, TT * (b + 1))
                    wait(dve, s_rr, b)
                    V.tensor_scalar(ms[:, :, :], ss[:, :, :], 1.0 / HD, NORM_EPS, ALU.mult, ALU.add).then_inc(s_ms, 1)
                    dve.wait_ge(s_rr, b + 1)
                    for t in range(TT):
                        wait(dve, s_rope, TT * b)
                        V.tensor_tensor(qn[:, t, :].rearrange("p (h d) -> p h d", d=HD),
                                        bank[t][:, :].rearrange("p (h d) -> p h d", d=HD),
                                        rr[:, t, :].rearrange("p (h o) -> p h o", o=1).to_broadcast([P, 2 * H, HD]),
                                        ALU.mult).then_inc(s_qn, 1)
                if cross:
                    split(2, i - 1, 1, 0)
                    split(2, i - 1, 0, 1)
                if self_:
                    split(1, i, 0, 0)
                    split(1, i, 1, 1)
                for a, b, on_ in ((2, i - 1, cross), (1, i, self_)):
                    if on_:
                        maxima(a, b)
                        max_t(a, b)
                for a, b, on_ in ((2, i - 1, cross), (1, i, self_)):
                    if on_:
                        for gr in range(NG):
                            out_t(a, b, gr)
                            if a == 1 and cross and gr == 1:
                                scale2(i - 1)
                        normalise_heads(a, b)
                        if a == 1:
                            dve.wait_ge(s_x0, 16 * (b + 1))
                            layer_norm(1, b, 1, x0)
                        else:
                            layer_norm(2, b, 1, xo[1])
                            if not self_:
                                scale2(b)
                if ffn:
                    dve.wait_ge(s_x2b, i - 2 + 1)
                    layer_norm(3, i - 2, FFN_BANK, x2b)

            dve.wait_ge(s_kb, 16)
            V.tensor_copy(maskf[:, :], maski[:, :]).then_inc(s_setup, 1)
            dve.wait_ge(s_setup, 1)
            V.tensor_scalar(maskf[:, :], maskf[:, :], 0.0, None, ALU.is_equal).then_inc(s_setup, 1)
            dve.wait_ge(s_setup, 2)
            V.tensor_scalar(maskb[:, :], maskf[:, :], BIG, None, ALU.mult).then_inc(s_setup, 1)
            for a in (1, 2):
                for s in range(2):
                    V.memset(stk[a][s][ROW_BIAS:K_ALL, :, :], 1.0).then_inc(s_setup, 1)
            dve.wait_ge(s_setup, 7)
            V.memset(stk[1][1][ROW_BIAS:ROW_BIAS + 1, :, :], 0.0).then_inc(s_setup, 1)
            dve.wait_ge(s_weights, 16 * N_WEIGHTS)
            for c in range(C):
                for which, lo, hi in ((0, 0, LIGHT * P), (1, LIGHT * P, FCH * P)):
                    V.tensor_scalar(w1[:, c, lo:hi], w1[:, c, lo:hi], gam[:, which, c:c + 1], float(D) ** 0.5,
                                    ALU.mult, ALU.mult).then_inc(s_setup, 1)
            V.tensor_tensor(b2sum[:, :], b2[:, 0, :], b2[:, 1, :], ALU.add).then_inc(s_setup, 1)
            h2 = HD // 2
            for t in range(TT):
                for s in range(2):
                    for half in range(2):
                        d = slice(half * h2, (half + 1) * h2)
                        V.tensor_tensor(ropeC[:, t, s, d], cs[:, t, 0, :], nw[:, s, d], ALU.mult).then_inc(s_setup, 1)
                    V.scalar_tensor_tensor(out=ropeS[:, t, s, 0:h2], in0=cs[:, t, 1, :], scalar=-1.0,
                                           in1=nw[:, s, h2:HD], op0=ALU.mult, op1=ALU.mult).then_inc(s_setup, 1)
                    V.tensor_tensor(ropeS[:, t, s, h2:HD], cs[:, t, 1, :], nw[:, s, 0:h2], ALU.mult).then_inc(s_setup, 1)
            iterations(dve, step)

        @block.gpsimd
        def _(pool):
            G = nc.gpsimd
            h2 = HD // 2

            def power(out, base, done, ready, b):
                pool.wait_ge(ready, b + 1)
                w = out.shape[-1]
                G.tensor_tensor(out, base, half_[:, 0, 0:w] if len(out.shape) == 2 else half_[:, :, :], ALU.pow)\
                    .then_inc(done, 1)

            def step(i, self_, cross, ffn):
                if self_:
                    b = i
                    wait(pool, s_qn, TT * b)
                    power(rr[:, :, :], ms[:, :, :], s_rr, s_ms, b)
                    for t in range(TT):
                        n = TT * b + t
                        pool.wait_ge(s_qn, n + 1)
                        wait(pool, s_nat[1], 2 * b)
                        four = "p (s h f d) -> p s h f d"
                        qv = qn[:, t, :].rearrange(four, s=2, h=H, f=2)
                        rv = rot[:, t, :].rearrange(four, s=2, h=H, f=2)
                        for s in range(2):
                            G.tensor_tensor(qr[:, t, s * D:(s + 1) * D].rearrange("p (h d) -> p h d", d=HD),
                                            qn[:, t, s * D:(s + 1) * D].rearrange("p (h d) -> p h d", d=HD),
                                            ropeC[:, t, s:s + 1, :].to_broadcast([P, H, HD]), ALU.mult)
                            for half in range(2):
                                last = G.tensor_tensor(rv[:, s, :, half, :], qv[:, s, :, 1 - half, :],
                                                       ropeS[:, t, s:s + 1, half * h2:(half + 1) * h2]
                                                       .to_broadcast([P, H, h2]), ALU.mult)
                        last.then_inc(s_rot, 1)
                        pool.wait_ge(s_rot, n + 1)
                        G.tensor_tensor(qr[:, t, :], qr[:, t, :], rot[:, t, :], ALU.add).then_inc(s_rope, 1)
                if ffn:
                    b = i - 2
                    pool.wait_ge(s_x[2], TT * (b + 1))
                    wait(pool, s_y[3], b)
                    G.tensor_tensor(x2b[:, :, :], xo[2][:, :, :],
                                    b2sum[:, :].rearrange("p (o d) -> p o d", o=1).to_broadcast([P, TT, D]),
                                    ALU.add).then_inc(s_x2b, 1)
                for a, b, on_ in ((2, i - 1, cross), (1, i, self_)):
                    if on_:
                        for h in range(H):
                            wait_apart(pool, (s_exp[a], H * b + h + 1))
                            slot = pr[:, h % (2 * HG), :].rearrange("p (k t) -> p k t", t=P)[:, 0:3:2, :]
                            G.affine_select(out=slot, in_=slot, compare_op=ALU.is_ge, fill=0.0, base=0,
                                            pattern=[[0, 2], [1, P]], channel_multiplier=-1).then_inc(s_prob[a], 1)
                            if a == 1 and cross and h == HG - 1:
                                power(rstd[2][:, :], ve[2][:, :], s_rs[2], s_ve[2], i - 1)
                            if a == 1 and cross and h == 3 * HG - 1:
                                power(rr2[:, :], ssm[:, :], s_sc2, s_ssm, i - 1)
                        if a == 2 and not self_:
                            power(rstd[2][:, :], ve[2][:, :], s_rs[2], s_ve[2], i - 1)
                            power(rr2[:, :], ssm[:, :], s_sc2, s_ssm, i - 1)
                        if a == 1:
                            power(rstd[1][:, :], ve[1][:, :], s_rs[1], s_ve[1], i)
                if ffn:
                    power(rstd[3][:, :], ve[3][:, :], s_rs[3], s_ve[3], i - 2)

            n = 0
            for m in (idf, idb):
                G.memset(m[:, :], 0.0).then_inc(s_pool, 1)
            G.memset(half_[:, :, :], -0.5)
            G.memset(cmask[:, :, :], 0.0).then_inc(s_pool, 1)
            for a in (1, 2):
                G.memset(va[a][:, :, :, :], 0.0).then_inc(s_pool, 1)
            pool.wait_ge(s_pool, 5)
            for m in (idf, idb):
                G.affine_select(out=m[:, :], in_=m[:, :], compare_op=ALU.not_equal, fill=1.0, base=0,
                                pattern=[[-1, P]], channel_multiplier=1)
            diag = cmask[:, 0:3:2, :]
            G.affine_select(out=diag, in_=diag, compare_op=ALU.is_ge, fill=BIG, base=0,
                            pattern=[[0, 2], [-1, P]], channel_multiplier=1)
            for a in (1, 2):
                last = G.memset(va[a][:, :, :, HD:HD + 1], 1.0)
            last.then_inc(s_const, 1)
            pool.wait_ge(s_setup, N_SETUP)
            iterations(pool, step)


N_WEIGHTS = 17
N_SETUP = 3 + 5 + 4 + 1 + TT * 2 * 4


def kernel(**inputs):
    import numpy as _np
    import concourse.bacc as _bacc
    from concourse import mybir as _mybir
    from concourse.bass_utils import run_bass_kernel_spmd as _run

    a = {k: _np.asarray(v) for k, v in inputs.items()}
    half = HD // 2
    freqs = _np.float32(32.0) ** (-_np.arange(0, HD, 2, dtype=_np.float32) / _np.float32(HD))
    angle = _np.arange(T, dtype=_np.float32)[:, None] * freqs[None, :].astype(_np.float32)
    arrays = {
        "x": a["x"], "xT": a["x"].transpose(0, 2, 1), "ctxT": a["ctx_1024"].transpose(0, 2, 1),
        "mask": a["mask_BxS2_if1"],
        "wqk1": a["L0_attn_w_qkv"][:2 * D].T, "wv1": a["L0_attn_w_qkv"][2 * D:].T, "wo1": a["L0_attn_w_proj"].T,
        "wq2": a["L0_xattn_Wq"], "wk2": a["L0_xattn_Wk"], "wv2": a["L0_xattn_Wv"], "wo2": a["L0_xattn_Wo"],
        "w1h": a["L0_ffn_w1_h"].T, "w1l": a["L0_ffn_w1_l"].T, "w2h": a["L0_ffn_w2_h"].T, "w2l": a["L0_ffn_w2_l"].T,
        "b1h": a["L0_ffn_b1_h"].reshape(FCH - 1, P).T, "b1l": a["L0_ffn_b1_l"].reshape(1, P).T,
        "gam": _np.stack([a["L0_ffn_gamma_h"].reshape(C, P), a["L0_ffn_gamma_l"].reshape(C, P)]).transpose(2, 0, 1),
        "b2": _np.stack([a["L0_ffn_b2_h"], a["L0_ffn_b2_l"]]),
        "nw": _np.stack([a["L0_attn_q_norm_w"], a["L0_attn_k_norm_w"]]),
        "cossin": _np.concatenate([_np.cos(angle), _np.sin(angle)], axis=1).astype(_np.float32),
    }
    nc = _bacc.Bacc("TRN2", target_bir_lowering=False, num_devices=1)
    feed, io = {}, {}
    for name, value in arrays.items():
        value = _np.ascontiguousarray(value)
        feed[f"in_{name}"] = value
        io[name] = nc.dram_tensor(f"in_{name}", value.shape, _mybir.dt.from_np(value.dtype), kind="ExternalInput").ap()
    io["out"] = nc.dram_tensor("out_x", (B, T, D), _mybir.dt.float32, kind="ExternalOutput").ap()
    build(nc, io)
    r = _run(nc, [feed], core_ids=[0])
    return r.results[0]["out_x"]
```

```python
from contextlib import ExitStack

import numpy as np
import concourse.bass as bass
from concourse import mybir

B, T, D, H = 16, 256, 256, 16
HD = D // H
P = 128
TT = T // P
C = D // P
HC = P // HD
TERMS_Q = (0, 0, 0, 1, 1, 2)
TERMS_K = (0, 1, 2, 0, 1, 0)
NPROD = len(TERMS_Q) * HD
ROW_BIAS = NPROD
ROW_MAX = NPROD + 1
K_MAX = ROW_MAX
K_ALL = ROW_MAX + 3
VW = 32
HG = 4
NG = H // HG
FCH = 9
LIGHT = FCH - 1
BIG = -1e30
NORM_EPS, LN_EPS = 1e-6, 1e-5


def build(nc, io):
    f32, bf16, i32 = mybir.dt.float32, mybir.dt.bfloat16, mybir.dt.int32
    ALU, ACT, AX = mybir.AluOpType, mybir.ActivationFunctionType, mybir.AxisListType
    ctx = ExitStack()
    with ctx:
        def sb(name, shape, dt=f32):
            return ctx.enter_context(nc.sbuf_tensor(name, shape, dt))

        def sem(name):
            return ctx.enter_context(nc.semaphore(name))

        wqk1 = sb("wqk1", [P, C, 2 * D]); wv1 = sb("wv1", [P, C, D]); wo1 = sb("wo1", [P, C, D])
        wq2 = sb("wq2", [P, C, D]); wk2 = sb("wk2", [P, C, D]); wv2 = sb("wv2", [P, C, D])
        wo2 = sb("wo2", [P, C, D])
        w1 = sb("w1", [P, C, FCH * P]); w2 = sb("w2", [P, FCH, D])
        b1 = sb("b1", [P, FCH]); b2 = sb("b2", [P, 2, D]); b2sum = sb("b2sum", [P, D])
        gam = sb("gam", [P, 2, C])
        cs = sb("cs", [P, TT, 2, HD // 2])
        nw = sb("nw", [P, 2, HD])
        ropeC = sb("ropeC", [P, TT, 2, HD]); ropeS = sb("ropeS", [P, TT, 2, HD])
        idf = sb("idf", [P, P]); idb = sb("idb", [P, P], bf16)
        cmask = sb("cmask", [P, 2, P], bf16)
        maski = sb("maski", [B, T], i32); maskf = sb("maskf", [B, T]); maskb = sb("maskb", [B, T], bf16)
        xT = sb("xT", [P, C, T]); ctxT = sb("ctxT", [P, C, T]); x1T = sb("x1T", [P, C, T])
        xnT = sb("xnT", [P, C, T])
        x0 = sb("x0", [P, TT, D]); x1c = sb("x1c", [P, TT, D])
        y = [None, sb("y1", [P, TT, D]), sb("y2", [P, TT, D]), sb("y3", [P, TT, D])]
        st = [None] + [sb(f"st{a}", [P, TT, 6]) for a in (1, 2, 3)]
        mv = [None] + [sb(f"mv{a}", [P, TT, 2]) for a in (1, 2, 3)]
        rstd = [None] + [sb(f"rstd{a}", [P, TT]) for a in (1, 2, 3)]
        ve = [None] + [sb(f"ve{a}", [P, TT]) for a in (1, 2, 3)]
        xo = [None, sb("x1", [P, TT, D]), sb("x2", [P, TT, D]), sb("x3", [P, TT, D])]
        sq = sb("sq", [P, TT, 2 * D]); ss = sb("ss", [P, TT, 2 * H]); rr = sb("rr", [P, TT, 2 * H]); ms = sb("ms", [P, TT, 2 * H]); nt = sb("nt", [P, TT, 2 * H])
        qn = sb("qn", [P, TT, 2 * D]); rot = sb("rot", [P, TT, 2 * D]); qc = sb("qc", [P, TT, 2 * D]); qr = sb("qr", [P, TT, 2 * D])
        sq2 = sb("sq2", [P, TT, D]); ss2 = sb("ss2", [P, TT]); xn = sb("xn", [P, TT, D])
        x2b = sb("x2b", [P, TT, D]); rr2 = sb("rr2", [P, TT]); ssm = sb("ssm", [P, TT])
        half_ = sb("half_", [P, TT, 2 * H])
        nat = [None] + [[sb(f"nat{a}{s}", [P, 3, C * T], bf16) for s in "qk"] for a in (1, 2)]
        rest = [None] + [[sb(f"rest{a}{s}", [P, C * T]) for s in "qk"] for a in (1, 2)]
        stk = [None] + [[sb(f"stk{a}{s}", [K_ALL, H, T], bf16) for s in "qk"] for a in (1, 2)]
        va = [None] + [sb(f"va{a}", [P, TT, H, VW]) for a in (1, 2)]
        mx = [None] + [sb(f"mx{a}", [P, H, 3]) for a in (1, 2)]
        nm = [None] + [sb(f"nm{a}", [P, TT, H]) for a in (1, 2)]
        nr = [None] + [sb(f"nr{a}", [P, TT, H]) for a in (1, 2)]
        mp = [None] + [sb(f"mp{a}", [P, TT, 3, H], bf16) for a in (1, 2)]
        mT = [None] + [sb(f"mT{a}", [3 * H, T], bf16) for a in (1, 2)]
        pr = sb("pr", [P, 2 * HG, 3 * P])
        oT = [None] + [sb(f"oT{a}", [P, NG, T]) for a in (1, 2)]
        rden = [None] + [sb(f"rden{a}", [P, TT, H]) for a in (1, 2)]
        on = [None] + [sb(f"on{a}", [P, TT, D]) for a in (1, 2)]
        onT = [None] + [sb(f"onT{a}", [P, C, T]) for a in (1, 2)]
        g = sb("g", [P, FCH, T])
        kb = nc.dram_tensor("kb", [B, T], bf16)

        bank = [ctx.enter_context(nc.psum_tensor(f"bank{i}", [P, 512], f32)) for i in range(8)]
        bankb = [bk[:, :].bitcast(bf16) for bk in bank]
        FFN_BANK, OT_BANK = 7, 6
        MAX_BANK, TOK_BANK, DIM_BANK, PROJ_BANK = (None, 0, 2), 2, 2, 3
        V_BANK = (None, 1, 4)
        S_BANKS, ST_BANKS = (0, 1, 6), (2, 3, 0)
        SPLIT_BANK = (None, (4, 5), (2, 5))

        def two(name):
            return [None, sem(name + "1"), sem(name + "2")]

        s_weights = sem("weights_loaded"); s_const = sem("consts_ready"); s_setup = sem("setup_step")
        s_kb = sem("keybias_stored"); s_pool = sem("pool_step")
        s_xT = sem("xT_loaded"); s_ctxT = sem("ctxT_loaded"); s_x0 = sem("x0_loaded")
        s_qk1 = sem("qk1_ready"); s_sq = sem("squares_ready"); s_ss = sem("dve_ss"); s_rr = sem("rr_ready"); s_ms = sem("meansq_ready")
        s_qn = sem("qn_ready"); s_rot = sem("pool_rot"); s_rope = sem("rope_ready")
        s_v = two("v_ready"); s_va = two("va_ready")
        s_nat = two("nat_ready"); s_hi = two("hi_ready"); s_rest = two("dve_rest"); s_mid = two("dve_mid")
        s_split = two("split_ready"); s_stk = two("stack_loaded")
        s_s = two("scores_ready"); s_mx = two("max_ready"); s_nm = two("dve_nm"); s_mp = two("maxparts_ready")
        s_mt = two("maxT_ready"); s_mT = two("maxT_copied"); s_ml = two("max_loaded")
        s_st = two("scoresT_ready"); s_exp = two("exp_ready"); s_prob = two("probs_ready")
        s_pv = two("out_ready"); s_oT = two("outT_copied"); s_ott = two("outtok_ready")
        s_rd = two("dve_rden"); s_on = two("on_ready"); s_ont = two("onT_ready"); s_onT = two("onT_copied")
        s_o = [None, sem("proj1_ready"), sem("proj2_ready"), sem("ffn_ready")]
        s_y = [None] + [sem(f"dve_y{a}") for a in (1, 2, 3)]
        s_bn = [None] + [sem(f"dve_bn{a}") for a in (1, 2, 3)]
        s_mv = [None] + [sem(f"dve_mv{a}") for a in (1, 2, 3)]
        s_rs = [None] + [sem(f"dve_rs{a}") for a in (1, 2, 3)]
        s_ve = [None] + [sem(f"var{a}_ready") for a in (1, 2, 3)]
        s_x = [None] + [sem(f"x{a}_ready") for a in (1, 2, 3)]
        s_x1t = sem("x1T_ready"); s_x1T = sem("x1T_copied")
        s_ss2 = sem("ss2_ready"); s_sc2 = sem("scale2_ready"); s_ssm = sem("ssm_ready"); s_xn = sem("xn_ready")
        s_xnt = sem("xnT_ready"); s_xnT = sem("xnT_copied"); s_x2b = sem("x2b_ready"); s_x1c = sem("x1c_ready"); s_new = sem("dve_newton")
        s_h = sem("hidden_ready"); s_g = sem("gelu_ready"); s_out = sem("out_stored")

        def wait(eng, s, value):
            if isinstance(value, int) and value <= 0:
                return
            eng.wait_ge(s, value)

        def wait_apart(eng, *waits):
            waits = [(s, v if isinstance(v, int) else eng.to_reg(v)) for s, v in waits]
            eng.wait_ge(s_const, 1)
            for s, value in waits:
                wait(eng, s, value)

        def live(b):
            return not isinstance(b, int) or 0 <= b < B

        def iterations(step, eng):
            for i in range(-1, 4):
                step(i)
            with eng.Fori(4, B - 2) as i:
                step(i)
            for i in range(B - 2, B + 3):
                step(i)

        block = ctx.enter_context(nc.Block())

        @block.sync
        def _(sp):
            def load(dst, src, s):
                sp.dma_start(dst, src).then_inc(s, 16)

            load(maski[:, :], io["mask"], s_kb)
            for dst, src in ((wqk1, io["wqk1"]), (wv1, io["wv1"]), (wo1, io["wo1"]), (wq2, io["wq2"]),
                             (wk2, io["wk2"]), (wv2, io["wv2"]), (wo2, io["wo2"]), (w1[:, :, 0:LIGHT * P], io["w1h"]),
                             (w1[:, :, LIGHT * P:FCH * P], io["w1l"]), (w2[:, 0:LIGHT, :], io["w2h"])):
                load(dst[:, :, :] if dst in (wqk1, wv1, wo1, wq2, wk2, wv2, wo2) else dst,
                     src.rearrange("(c p) n -> p c n", p=P), s_weights)
            load(w2[:, LIGHT, :], io["w2l"], s_weights)
            load(b1[:, 0:LIGHT], io["b1h"], s_weights)
            load(b1[:, LIGHT:FCH], io["b1l"], s_weights)
            load(gam[:, :, :], io["gam"], s_weights)
            load(cs[:, :, :, :], io["cossin"].rearrange("(t p) (s d) -> p t s d", p=P, s=2), s_weights)
            load(b2[:, :, :], io["b2"].rearrange("(o s) d -> o s d", o=1).to_broadcast([P, 2, D]), s_weights)
            load(nw[:, :, :], io["nw"].rearrange("(o s) d -> o s d", o=1).to_broadcast([P, 2, HD]), s_weights)
            sp.wait_ge(s_setup, 3)
            load(kb.ap(), maskb[:, :], s_kb)
            sp.wait_ge(s_kb, 32)

            def stacks(a, b):
                wait_apart(sp, (s_pv[a], NG * b))
                if a == 2:
                    load(stk[2][1][ROW_BIAS:ROW_BIAS + 1, :, :],
                         kb.ap()[bass.ds(b, 1), :].rearrange("o (h t) -> o h t", h=1).to_broadcast([1, H, T]), s_stk[2])
                for nth, s in enumerate((None, (0, 1), (1, 0))[a]):
                    wait_apart(sp, (s_split[a], 2 * b + nth + 1))
                    for r, part in enumerate((TERMS_Q, TERMS_K)[s]):
                        load(stk[a][s][r * HD:(r + 1) * HD, :, :], nat[a][s][:, part, :], s_stk[a])

            def maxima(a, b):
                wait_apart(sp, (s_mT[a], b + 1))
                load(stk[a][0][ROW_MAX:ROW_MAX + 3, :, :], mT[a][:, :], s_ml[a])

            def tokens(dram, b):
                return dram[bass.ds(b, 1)].rearrange("o (t p) d -> p (o t) d", p=P)

            def dims(dram, b):
                return dram[bass.ds(b, 1)].rearrange("o (c p) t -> p (o c) t", p=P)

            def step(i):
                if live(i):
                    wait_apart(sp, (s_y[1], i))
                    load(x0[:, :, :], tokens(io["x"], i), s_x0)
                    maxima(1, i)
                if live(i - 1):
                    stacks(2, i - 1)
                if live(i):
                    wait_apart(sp, (s_v[2], i))
                    load(ctxT[:, :, :], dims(io["ctxT"], i), s_ctxT)
                if live(i - 3):
                    wait_apart(sp, (s_x[3], TT * (i - 2)))
                    load(tokens(io["out"], i - 3), xo[3][:, :, :], s_out)
                if live(i - 1):
                    maxima(2, i - 1)
                if live(i + 1):
                    stacks(1, i + 1)
                if live(i + 2):
                    wait_apart(sp, (s_v[1], i + 2))
                    load(xT[:, :, :], dims(io["xT"], i + 2), s_xT)

            load(xT[:, :, :], dims(io["xT"], 0), s_xT)
            iterations(step, sp)
            sp.wait_ge(s_out, 16 * B)

        @block.tensor
        def _(pe):
            def mm(out, lhsT, rhs, start, stop, check=False):
                return nc.tensor.matmul(out, lhsT, rhs, start=start, stop=stop, skip_group_check=check)

            def tok_proj(out, src, t, w, lo, n):
                for c in range(C):
                    last = mm(out, src[:, c, t * P:(t + 1) * P], w[:, c, lo:lo + n], c == 0, c == C - 1)
                return last

            def dim_proj(out, w, lo, src):
                for c in range(C):
                    last = mm(out, w[:, c, lo:lo + P], src[:, c, :], c == 0, c == C - 1)
                return last

            def four_transposes(k, src):
                for c in range(C):
                    for t in range(TT):
                        last = nc.tensor.transpose(bank[k][:, c * T + t * P:c * T + (t + 1) * P],
                                                   src[:, t, c * P:(c + 1) * P], idf[:, :])
                return last

            def qk1(b, t):
                if t == 0:
                    pe.wait_ge(s_xT, 16 * (b + 1))
                else:
                    wait(pe, s_va[2], b - 1)
                tok_proj(bank[(1, 4)[t]][:, :], xT, t, wqk1, 0, 2 * D).then_inc(s_qk1, 1)

            def v1(b):
                wait(pe, s_mx[2], H * (b - 2) + 14 if live(b - 2) else 0)
                for t in range(TT):
                    last = tok_proj(bank[V_BANK[1]][:, t * D:(t + 1) * D], xT, t, wv1, 0, D)
                last.then_inc(s_v[1], 1)

            def transpose_x1(b):
                pe.wait_ge(s_x[1], TT * (b + 1))
                if live(b + 1):
                    pe.wait_ge(s_mx[1], H * (b + 2))
                four_transposes(6, xo[1]).then_inc(s_x1t, 1)

            def k2(b):
                for c in range(C):
                    last = dim_proj(bank[5][:, c * T:(c + 1) * T], wk2, c * P, ctxT)
                last.then_inc(s_nat[2], 1)

            def v2(b):
                pe.wait_ge(s_ctxT, 16 * (b + 1))
                if live(b + 1):
                    pe.wait_ge(s_rest[1], 2 * (b + 2))
                for t in range(TT):
                    last = tok_proj(bank[V_BANK[2]][:, t * D:(t + 1) * D], ctxT, t, wv2, 0, D)
                last.then_inc(s_v[2], 1)

            def q2(b):
                pe.wait_ge(s_x1T, b + 1)
                for c in range(C):
                    last = dim_proj(bank[2][:, c * T:(c + 1) * T], wq2, c * P, x1T)
                last.then_inc(s_nat[2], 1)

            def transpose_xn(b):
                pe.wait_ge(s_xn, TT * (b + 1))
                if live(b + 1):
                    pe.wait_ge(s_rest[2], 2 * (b + 1) + 1)
                four_transposes(5, xn).then_inc(s_xnt, 1)

            def hidden(b, j):
                k = 4 + j % 2
                if j == 0:
                    pe.wait_ge(s_xnT, b + 1)
                    if live(b + 3):
                        pe.wait_ge(s_qn, TT * (b + 4))
                elif j >= 2:
                    pe.wait_ge(s_g, FCH * b + j - 1)
                dim_proj(bank[k][:, 0:T], w1, j * P, xnT).then_inc(s_h, 1)

            def transpose_qk1(b):
                pe.wait_ge(s_rope, TT * (b + 1))
                wait(pe, s_g, FCH * (b - 2))
                for s in range(2):
                    four_transposes(4 + s, qr[:, :, s * D:(s + 1) * D]).then_inc(s_nat[1], 1)

            def scores(a, b, h):
                if h == 0:
                    pe.wait_ge(s_stk[a], 16 * NSTK[a] * (b + 1))
                    if live((b - 2, b + 1)[a - 1]):
                        pe.wait_ge(s_exp[3 - a], H * (b - 2, b + 1)[a - 1] + 15)
                if h == 1 and a == 1:
                    pe.wait_ge(s_va[1], b + 1)
                if h == 1 and a == 2 and live(b + 2):
                    pe.wait_ge(s_qn, TT * (b + 2) + 1)
                if h == 2 and live((b - 2, b + 1)[a - 1]):
                    pe.wait_ge(s_oT[3 - a], NG * (b - 1, b + 2)[a - 1])
                if h >= 3:
                    pe.wait_ge(s_mx[a], H * b + h - 2)
                k = S_BANKS[h % 3]
                q, kk = stk[a]
                blocks = bank[k][:, 0:3 * P].rearrange("p (k t) -> p k t", k=3)
                mm(blocks[:, 0:3:2, :], idb[:, :], cmask[:, :, :], True, False, True)
                mm(bank[k][:, 0:P], q[0:K_MAX, h, 0:P], kk[0:K_MAX, h, 0:P], False, False, True)
                mm(bank[k][:, P:3 * P], q[0:K_MAX, h, P:T], kk[0:K_MAX, h, :], False, True, True).then_inc(s_s[a], 1)

            def transpose_max(a, b):
                wait_apart(pe, (s_mp[a], b + 1))
                for t in range(TT):
                    last = nc.tensor.transpose(bankb[MAX_BANK[a]][0:3 * H, t * P:(t + 1) * P], mp[a][:, t, :, :], idb[:, :])
                last.then_inc(s_mt[a], 1)

            def scores_t(a, b, h):
                if h == 0:
                    pe.wait_ge(s_ml[a], 16 * (b + 1))
                    if a == 1:
                        wait(pe, s_rest[2], 2 * b)
                if h == 1:
                    if a == 2 and live(b + 1):
                        pe.wait_ge(s_y[1], b + 2)
                    if a == 1:
                        wait(pe, s_y[2], b - 1)
                k = ST_BANKS[h % 3]
                if h >= 3:
                    pe.wait_ge(s_exp[a], H * b + h - 2)
                q, kk = stk[a]
                mm(bank[k][:, 0:T], kk[0:K_ALL, h, 0:P], q[0:K_ALL, h, :], True, True)
                mm(bank[k][:, T:3 * P], kk[0:K_ALL, h, P:T], q[0:K_ALL, h, P:T], True, True).then_inc(s_st[a], 1)

            def values(a, b, gr):
                pe.wait_ge(s_prob[a], H * b + HG * (gr + 1))
                if gr > 0:
                    pe.wait_ge(s_oT[a], NG * b + gr)
                for key in range(2):
                    for j in range(HG):
                        h = HG * gr + j
                        out = bank[OT_BANK][VW * j:VW * (j + 1), :]
                        if key == 0:
                            mm(out[:, 0:T], va[a][:, 0, h, :], pr[:, h % (2 * HG), 0:T], True, False, True)
                        else:
                            last = mm(out[:, P:T], va[a][:, 1, h, :], pr[:, h % (2 * HG), T:3 * P], False, True, True)
                last.then_inc(s_pv[a], 1)

            def out_tokens(a, b):
                pe.wait_ge(s_oT[a], NG * (b + 1))
                for t in range(TT):
                    for gr in range(NG):
                        last = nc.tensor.transpose(bank[TOK_BANK + t][:, gr * P:(gr + 1) * P],
                                                   oT[a][:, gr, t * P:(t + 1) * P], idf[:, :])
                    last.then_inc(s_ott[a], 1)

            def out_dims(a, b):
                pe.wait_ge(s_on[a], TT * (b + 1))
                four_transposes(DIM_BANK, on[a]).then_inc(s_ont[a], 1)

            def out_proj(a, b):
                pe.wait_ge(s_onT[a], b + 1)
                for t in range(TT):
                    last = tok_proj(bank[PROJ_BANK][:, t * D:(t + 1) * D], onT[a], t, (None, wo1, wo2)[a], 0, D)
                last.then_inc(s_o[a], 1)

            def ffn_out(b, t, j):
                if t == 0 and j == 0:
                    wait(pe, s_y[3], b)
                if t == 0:
                    pe.wait_ge(s_g, FCH * b + j + 1)
                last = mm(bank[FFN_BANK][:, t * D:(t + 1) * D], g[:, j, t * P:(t + 1) * P], w2[:, j, :],
                          j == 0, j == FCH - 1)
                if t == TT - 1 and j == FCH - 1:
                    last.then_inc(s_o[3], 1)

            def phase(heads, others):
                for h in range(H + 1):
                    for other in others.get(h, []):
                        other()
                    if heads and h < H:
                        heads(h)

            def step(i):
                s, c, f, l = i, i - 1, i - 2, i - 3
                others = {}

                def add(at, fn, *args):
                    others.setdefault(at, []).append(lambda: fn(*args))

                if live(f):
                    add(2, values, 2, f, NG - 1)
                    add(3, out_tokens, 2, f)
                    add(9, out_dims, 2, f)
                    add(14, out_proj, 2, f)
                if live(c):
                    add(6, v2, c)
                phase((lambda h: scores(1, s, h)) if live(s) else None, others)
                if live(c):
                    k2(c)
                if live(s):
                    transpose_max(1, s)
                if live(c):
                    transpose_x1(c)
                if live(i + 1):
                    qk1(i + 1, 0)
                if live(c):
                    q2(c)
                if live(i + 1):
                    qk1(i + 1, 1)
                others = {}
                if live(l):
                    for j in range(FCH):
                        add(2 * j if j < 8 else H - 1, ffn_out, l, 1, j)
                if live(f):
                    add(9, transpose_xn, f)
                if live(s):
                    for gr in range(NG - 1):
                        add(HG * gr + VALUES_AFTER, values, 1, s, gr)
                phase((lambda h: scores_t(1, s, h)) if live(s) else None, others)
                others = {}
                if live(s):
                    add(2, values, 1, s, NG - 1)
                    add(4, out_tokens, 1, s)
                    add(8, out_dims, 1, s)
                    add(12, out_proj, 1, s)
                if live(f):
                    for j in range(FCH):
                        add(1 + 3 * j // 2, hidden, f, j)
                phase((lambda h: scores(2, c, h)) if live(c) else None, others)
                if live(i + 1):
                    transpose_qk1(i + 1)
                    v1(i + 1)
                if live(c):
                    transpose_max(2, c)
                others = {}
                if live(f):
                    for j in range(FCH):
                        add(0 if j < FILL_M2 else 3 * (j - FILL_M2) + 1, ffn_out, f, 0, j)
                if live(c):
                    for gr in range(NG - 1):
                        add(HG * gr + VALUES_AFTER, values, 2, c, gr)
                phase((lambda h: scores_t(2, c, h)) if live(c) else None, others)

            pe.wait_ge(s_weights, 16 * N_WEIGHTS)
            pe.wait_ge(s_const, 1)
            pe.wait_ge(s_setup, N_SETUP)
            iterations(step, pe)

        @block.scalar
        def _(act):
            def copy(out, in_):
                return nc.scalar.activation(out, in_, ACT.Copy)

            def copy_v(a, b):
                act.wait_ge(s_v[a], b + 1)
                wait(act, s_pv[a], NG * b)
                copy(va[a][:, :, :, 0:HD], bank[V_BANK[a]][:, :].rearrange("p (t h d) -> p t h d", t=TT, h=H))\
                    .then_inc(s_va[a], 1)

            def copy_dims(dst, k):
                return copy(dst[:, :, :], bank[k][:, :].rearrange("p (c t) -> p c t", c=C))

            def copy_out(a, b):
                act.wait_ge(s_ont[a], b + 1)
                copy_dims(onT[a], DIM_BANK).then_inc(s_onT[a], 1)

            def copy_group(a, b, gr):
                act.wait_ge(s_pv[a], NG * b + gr + 1)
                wait(act, s_ott[a], TT * b)
                copy(oT[a][:, gr, :], bank[OT_BANK][:, 0:T]).then_inc(s_oT[a], 1)

            def exponentials(a, b, h):
                if h % HG == 0 and h >= 2 * HG:
                    copy_group(a, b, h // HG - 2)
                act.wait_ge(s_st[a], H * b + h + 1)
                if h >= 2 * HG:
                    act.wait_ge(s_pv[a], NG * b + h // HG - 1)
                else:
                    if a == 1:
                        wait(act, s_pv[2], NG * (b - 1) - 1 + h // HG)
                    elif live(b + 1):
                        act.wait_ge(s_pv[1], NG * (b + 2) - 1 + h // HG)
                    else:
                        act.wait_ge(s_pv[2], NG * b - 1 + h // HG)
                nc.scalar.activation(pr[:, h % (2 * HG), :], bank[ST_BANKS[h % 3]][:, 0:3 * P], ACT.Exp, scale=HD ** -0.5)\
                    .then_inc(s_exp[a], 1)
                if h == H - 1:
                    copy_group(a, b, NG - 2)
                    copy_group(a, b, NG - 1)

            def step(i):
                s, c, f = i, i - 1, i - 2
                if live(c):
                    copy_v(2, c)
                if live(f):
                    copy_out(2, f)
                if live(c):
                    high_part(2, c, 1, 0)
                    act.wait_ge(s_x1t, c + 1)
                    wait(act, s_nat[2], 2 * c)
                    copy_dims(x1T, 6).then_inc(s_x1T, 1)
                if live(f):
                    norms(f)
                if live(c):
                    high_part(2, c, 0, 1)
                if live(i + 1):
                    b = i + 1
                    for t in range(TT):
                        act.wait_ge(s_qk1, TT * b + t + 1)
                        wait(act, s_ss, TT * b)
                        nc.scalar.activation(sq[:, t, :], bank[(1, 4)[t]][:, :], ACT.Square).then_inc(s_sq, 1)
                for h in range(H):
                    if h == 11 and live(f):
                        act.wait_ge(s_xnt, f + 1)
                        wait(act, s_h, FCH * f)
                        copy_dims(xnT, 5).then_inc(s_xnT, 1)
                    if live(s):
                        exponentials(1, s, h)
                for j in range(FCH):
                    if live(f):
                        act.wait_ge(s_h, FCH * f + j + 1)
                        if j == 0:
                            wait(act, s_o[3], f)
                        nc.scalar.activation(g[:, j, :], bank[4 + j % 2][:, 0:T], ACT.Gelu, bias=b1[:, j:j + 1])\
                            .then_inc(s_g, 1)
                    if j == 4 and live(s):
                        copy_out(1, s)
                if live(i + 1):
                    high_part(1, i + 1, 0, 0)
                    high_part(1, i + 1, 1, 1)
                    copy_v(1, i + 1)
                if live(c):
                    for h in range(H):
                        exponentials(2, c, h)

            def norms(b):
                wait(act, s_ssm, b)
                for t in range(TT):
                    act.wait_ge(s_x[2], TT * b + t + 1)
                    nc.scalar.activation(sq2[:, t, :], xo[2][:, t, :], ACT.Square,
                                         accum_out=ss2[:, t:t + 1]).then_inc(s_ss2, 1)

            def high_part(a, b, s, nth):
                act.wait_ge(s_nat[a], 2 * b + nth + 1)
                wait(act, s_stk[a], 16 * NSTK[a] * b)
                copy(nat[a][s][:, 0, :], bank[SPLIT_BANK[a][s]][:, :]).then_inc(s_hi[a], 1)

            act.wait_ge(s_weights, 16 * N_WEIGHTS)
            iterations(step, act)

        @block.vector
        def _(dve):
            V = nc.vector

            def split(a, b, s, nth):
                dve.wait_ge(s_hi[a], 2 * b + nth + 1)
                n = nat[a][s]
                V.tensor_tensor(rest[a][s][:, :], bank[SPLIT_BANK[a][s]][:, :], n[:, 0, :], ALU.subtract)\
                    .then_inc(s_rest[a], 1)
                dve.wait_ge(s_rest[a], 2 * b + nth + 1)
                V.tensor_copy(n[:, 1, :], rest[a][s][:, :]).then_inc(s_mid[a], 1)
                dve.wait_ge(s_mid[a], 2 * b + nth + 1)
                V.tensor_tensor(n[:, 2, :], rest[a][s][:, :], n[:, 1, :], ALU.subtract).then_inc(s_split[a], 1)

            def maxima(a, b, between):
                for h in range(H):
                    if h in between:
                        between[h]()
                    dve.wait_ge(s_s[a], H * b + h + 1)
                    V.tensor_reduce(mx[a][:, h, :], bank[S_BANKS[h % 3]][:, 0:3 * P].rearrange("p (k t) -> p k t", k=3),
                                    AX.X, ALU.max, negate=True).then_inc(s_mx[a], 1)
                dve.wait_ge(s_mx[a], H * (b + 1))
                V.tensor_copy(nm[a][:, 0, :], mx[a][:, :, 0])
                V.tensor_tensor(nm[a][:, 1, :], mx[a][:, :, 1], mx[a][:, :, 2], ALU.min).then_inc(s_nm[a], 1)
                dve.wait_ge(s_nm[a], 4 * b + 1)
                wait(dve, s_mt[a], b)
                V.tensor_copy(mp[a][:, :, 0, :], nm[a][:, :, :]).then_inc(s_nm[a], 1)
                dve.wait_ge(s_nm[a], 4 * b + 2)
                V.tensor_tensor(nr[a][:, :, :], nm[a][:, :, :], mp[a][:, :, 0, :], ALU.subtract).then_inc(s_nm[a], 1)
                dve.wait_ge(s_nm[a], 4 * b + 3)
                V.tensor_copy(mp[a][:, :, 1, :], nr[a][:, :, :]).then_inc(s_nm[a], 1)
                dve.wait_ge(s_nm[a], 4 * b + 4)
                V.tensor_tensor(mp[a][:, :, 2, :], nr[a][:, :, :], mp[a][:, :, 1, :], ALU.subtract).then_inc(s_mp[a], 1)

            def max_t(a, b):
                dve.wait_ge(s_mt[a], b + 1)
                wait(dve, s_ml[a], 16 * b)
                V.tensor_copy(mT[a][:, :], bankb[MAX_BANK[a]][0:3 * H, 0:T]).then_inc(s_mT[a], 1)

            def normalise_heads(a, b):
                for t in range(TT):
                    dve.wait_ge(s_ott[a], TT * b + t + 1)
                    o = bank[TOK_BANK + t][:, :].rearrange("p (h w) -> p h w", w=VW)
                    V.reciprocal(rden[a][:, t, :], o[:, :, HD]).then_inc(s_rd[a], 1)
                    dve.wait_ge(s_rd[a], TT * b + t + 1)
                    wait(dve, s_ont[a], b)
                    V.tensor_tensor(on[a][:, t, :].rearrange("p (h d) -> p h d", d=HD), o[:, :, 0:HD],
                                    rden[a][:, t, :].rearrange("p (h o) -> p h o", o=1).to_broadcast([P, H, HD]),
                                    ALU.mult).then_inc(s_on[a], 1)

            def add_residual(a, b, k, resid):
                dve.wait_ge(s_o[a], b + 1)
                wait(dve, s_x[a], TT * b)
                V.tensor_tensor(y[a][:, :, :], bank[k][:, :].rearrange("p (t d) -> p t d", t=TT), resid[:, :, :], ALU.add)\
                    .then_inc(s_y[a], 1)

            def layer_norm(a, b):
                dve.wait_ge(s_y[a], b + 1)
                for t in range(TT):
                    V.bn_stats(st[a][:, t, :], y[a][:, t, :]).then_inc(s_bn[a], 1)
                for t in range(TT):
                    wait_apart(dve, (s_bn[a], TT * b + t + 1))
                    V.bn_aggr(mv[a][:, t, :], st[a][:, t, :]).then_inc(s_mv[a], 1)
                dve.wait_ge(s_mv[a], TT * (b + 1))
                wait(dve, s_rs[a], b)
                V.tensor_scalar(ve[a][:, :], mv[a][:, :, 1], LN_EPS, None, ALU.add).then_inc(s_ve[a], 1)
                dve.wait_ge(s_rs[a], b + 1)
                if a == 1:
                    wait(dve, s_x1t, b)
                    wait(dve, s_x1c, b)
                elif a == 2:
                    wait(dve, s_x2b, b)
                else:
                    wait(dve, s_out, 16 * b)
                for t in range(TT):
                    V.tensor_scalar(xo[a][:, t, :], y[a][:, t, :], mv[a][:, t, 0:1], rstd[a][:, t:t + 1],
                                    ALU.subtract, ALU.mult).then_inc(s_x[a], 1)

            def scale2(b):
                dve.wait_ge(s_ss2, TT * (b + 1))
                wait(dve, s_sc2, b)
                V.tensor_scalar(ssm[:, :], ss2[:, :], 1e-24, None, ALU.max).then_inc(s_ssm, 1)
                dve.wait_ge(s_sc2, b + 1)
                wait(dve, s_xnt, b)
                for t in range(TT):
                    V.tensor_scalar(xn[:, t, :], xo[2][:, t, :], rr2[:, t:t + 1], None, ALU.mult).then_inc(s_xn, 1)

            def scaled_qk(b):
                for t in range(TT):
                    dve.wait_ge(s_sq, TT * b + t + 1)
                    V.tensor_reduce(ss[:, t, :], sq[:, t, :].rearrange("p (h d) -> p h d", d=HD), AX.X, ALU.add)\
                        .then_inc(s_ss, 1)
                dve.wait_ge(s_ss, TT * (b + 1))
                n = NEWTON * b
                V.tensor_scalar(ms[:, :, :], ss[:, :, :], 1.0 / HD, NORM_EPS, ALU.mult, ALU.add).then_inc(s_new, 1)
                dve.wait_ge(s_new, n + 1)
                V.tensor_scalar(nt[:, :, :].bitcast(i32), ms[:, :, :].bitcast(i32), 1, None, ALU.logical_shift_right)\
                    .then_inc(s_new, 1)
                dve.wait_ge(s_new, n + 2)
                V.tensor_scalar(rr[:, :, :].bitcast(i32), nt[:, :, :].bitcast(i32), -1.0, float(0x5F3759DF),
                                ALU.mult, ALU.add).then_inc(s_new, 1)
                for k in range(3):
                    dve.wait_ge(s_new, n + 3 * k + 3)
                    V.tensor_tensor(nt[:, :, :], rr[:, :, :], rr[:, :, :], ALU.mult).then_inc(s_new, 1)
                    dve.wait_ge(s_new, n + 3 * k + 4)
                    V.scalar_tensor_tensor(out=nt[:, :, :], in0=ms[:, :, :], scalar=-0.5, in1=nt[:, :, :],
                                           op0=ALU.mult, op1=ALU.mult).then_inc(s_new, 1)
                    dve.wait_ge(s_new, n + 3 * k + 5)
                    V.scalar_tensor_tensor(out=rr[:, :, :], in0=nt[:, :, :], scalar=1.5, in1=rr[:, :, :],
                                           op0=ALU.add, op1=ALU.mult).then_inc(s_new, 1)
                dve.wait_ge(s_new, n + NEWTON)
                for t in range(TT):
                    wait(dve, s_rope, TT * b)
                    V.tensor_tensor(qn[:, t, :].rearrange("p (h d) -> p h d", d=HD),
                                    bank[(1, 4)[t]][:, :].rearrange("p (h d) -> p h d", d=HD),
                                    rr[:, t, :].rearrange("p (h o) -> p h o", o=1).to_broadcast([P, 2 * H, HD]),
                                    ALU.mult).then_inc(s_qn, 1)

            def step(i):
                s, c, f, l = i, i - 1, i - 2, i - 3
                if live(s):
                    maxima(1, s, {4: lambda: normalise_heads(2, f)} if live(f) else {})
                elif live(f):
                    normalise_heads(2, f)
                if live(s):
                    max_t(1, s)
                if live(f):
                    dve.wait_ge(s_x1c, f + 1)
                    add_residual(2, f, PROJ_BANK, x1c)
                if live(f):
                    layer_norm(2, f)
                if live(c):
                    split(2, c, 1, 0)
                if live(f):
                    scale2(f)
                if live(c):
                    split(2, c, 0, 1)
                if live(i + 1):
                    scaled_qk(i + 1)
                if live(l):
                    dve.wait_ge(s_x2b, l + 1)
                    add_residual(3, l, FFN_BANK, x2b)
                    layer_norm(3, l)
                if live(c):
                    maxima(2, c, {5: lambda: normalise_heads(1, s)} if live(s) else {})
                elif live(s):
                    normalise_heads(1, s)
                if live(i + 1):
                    split(1, i + 1, 0, 0)
                if live(c):
                    max_t(2, c)
                if live(s):
                    dve.wait_ge(s_x0, 16 * (s + 1))
                    add_residual(1, s, PROJ_BANK, x0)
                if live(i + 1):
                    split(1, i + 1, 1, 1)
                if live(s):
                    layer_norm(1, s)
            dve.wait_ge(s_kb, 16)
            V.tensor_copy(maskf[:, :], maski[:, :]).then_inc(s_setup, 1)
            dve.wait_ge(s_setup, 1)
            V.tensor_scalar(maskf[:, :], maskf[:, :], 0.0, None, ALU.is_equal).then_inc(s_setup, 1)
            dve.wait_ge(s_setup, 2)
            V.tensor_scalar(maskb[:, :], maskf[:, :], BIG, None, ALU.mult).then_inc(s_setup, 1)
            for a in (1, 2):
                for s in range(2):
                    V.memset(stk[a][s][ROW_BIAS:K_ALL, :, :], 1.0).then_inc(s_setup, 1)
            dve.wait_ge(s_setup, 7)
            V.memset(stk[1][1][ROW_BIAS:ROW_BIAS + 1, :, :], 0.0).then_inc(s_setup, 1)
            dve.wait_ge(s_weights, 16 * N_WEIGHTS)
            for c in range(C):
                for which, lo, hi in ((0, 0, LIGHT * P), (1, LIGHT * P, FCH * P)):
                    V.tensor_scalar(w1[:, c, lo:hi], w1[:, c, lo:hi], gam[:, which, c:c + 1], float(D) ** 0.5,
                                    ALU.mult, ALU.mult).then_inc(s_setup, 1)
            V.tensor_tensor(b2sum[:, :], b2[:, 0, :], b2[:, 1, :], ALU.add).then_inc(s_setup, 1)
            h2 = HD // 2
            for t in range(TT):
                for s in range(2):
                    for half in range(2):
                        d = slice(half * h2, (half + 1) * h2)
                        V.tensor_tensor(ropeC[:, t, s, d], cs[:, t, 0, :], nw[:, s, d], ALU.mult).then_inc(s_setup, 1)
                    V.scalar_tensor_tensor(out=ropeS[:, t, s, 0:h2], in0=cs[:, t, 1, :], scalar=-1.0,
                                           in1=nw[:, s, h2:HD], op0=ALU.mult, op1=ALU.mult).then_inc(s_setup, 1)
                    V.tensor_tensor(ropeS[:, t, s, h2:HD], cs[:, t, 1, :], nw[:, s, 0:h2], ALU.mult).then_inc(s_setup, 1)
            iterations(step, dve)

        @block.gpsimd
        def _(pool):
            G = nc.gpsimd
            h2 = HD // 2

            def power(out, base, done, ready, b):
                pool.wait_ge(ready, b + 1)
                w = out.shape[-1]
                G.tensor_tensor(out, base, half_[:, 0, 0:w] if len(out.shape) == 2 else half_[:, :, :], ALU.pow)\
                    .then_inc(done, 1)

            def rotate(b):
                for t in range(TT):
                    n = TT * b + t
                    pool.wait_ge(s_qn, n + 1)
                    wait(pool, s_nat[1], 2 * b)
                    four = "p (s h f d) -> p s h f d"
                    qv = qn[:, t, :].rearrange(four, s=2, h=H, f=2)
                    rv = rot[:, t, :].rearrange(four, s=2, h=H, f=2)
                    for s in range(2):
                        G.tensor_tensor(qc[:, t, s * D:(s + 1) * D].rearrange("p (h d) -> p h d", d=HD),
                                        qn[:, t, s * D:(s + 1) * D].rearrange("p (h d) -> p h d", d=HD),
                                        ropeC[:, t, s:s + 1, :].to_broadcast([P, H, HD]), ALU.mult)
                        for half in range(2):
                            last = G.tensor_tensor(rv[:, s, :, half, :], qv[:, s, :, 1 - half, :],
                                                   ropeS[:, t, s:s + 1, half * h2:(half + 1) * h2]
                                                   .to_broadcast([P, H, h2]), ALU.mult)
                    last.then_inc(s_rot, 1)
                    pool.wait_ge(s_rot, n + 1)
                    for s in range(2):
                        pairs = "p (j c d) -> p j c d"
                        last = G.tensor_tensor(qr[:, t, s * D:(s + 1) * D].rearrange("p (c d j) -> p j c d", c=C, d=HD),
                                               qc[:, t, s * D:(s + 1) * D].rearrange(pairs, c=C, d=HD),
                                               rot[:, t, s * D:(s + 1) * D].rearrange(pairs, c=C, d=HD), ALU.add)
                    last.then_inc(s_rope, 1)

            def mask_probs(a, b):
                for h in range(H):
                    wait_apart(pool, (s_exp[a], H * b + h + 1))
                    slot = pr[:, h % (2 * HG), :].rearrange("p (k t) -> p k t", t=P)[:, 0:3:2, :]
                    G.affine_select(out=slot, in_=slot, compare_op=ALU.is_ge, fill=0.0, base=0,
                                    pattern=[[0, 2], [1, P]], channel_multiplier=-1).then_inc(s_prob[a], 1)

            def step(i):
                s, c, f, l = i, i - 1, i - 2, i - 3
                if live(f):
                    power(rstd[2][:, :], ve[2][:, :], s_rs[2], s_ve[2], f)
                    power(rr2[:, :], ssm[:, :], s_sc2, s_ssm, f)
                if live(c):
                    wait_apart(pool, (s_x[1], TT * (c + 1)), (s_y[2], c))
                    G.tensor_copy(x1c[:, :, :], xo[1][:, :, :]).then_inc(s_x1c, 1)
                if live(s):
                    mask_probs(1, s)
                if live(l):
                    power(rstd[3][:, :], ve[3][:, :], s_rs[3], s_ve[3], l)
                if live(i + 1):
                    rotate(i + 1)
                if live(f):
                    pool.wait_ge(s_x[2], TT * (f + 1))
                    wait(pool, s_y[3], f)
                    G.tensor_tensor(x2b[:, :, :], xo[2][:, :, :],
                                    b2sum[:, :].rearrange("p (o d) -> p o d", o=1).to_broadcast([P, TT, D]),
                                    ALU.add).then_inc(s_x2b, 1)
                if live(s):
                    power(rstd[1][:, :], ve[1][:, :], s_rs[1], s_ve[1], s)
                if live(c):
                    mask_probs(2, c)

            n = 0
            for m in (idf, idb):
                G.memset(m[:, :], 0.0).then_inc(s_pool, 1)
            G.memset(half_[:, :, :], -0.5)
            G.memset(cmask[:, :, :], 0.0).then_inc(s_pool, 1)
            for a in (1, 2):
                G.memset(va[a][:, :, :, :], 0.0).then_inc(s_pool, 1)
            pool.wait_ge(s_pool, 5)
            for m in (idf, idb):
                G.affine_select(out=m[:, :], in_=m[:, :], compare_op=ALU.not_equal, fill=1.0, base=0,
                                pattern=[[-1, P]], channel_multiplier=1)
            diag = cmask[:, :, :]
            G.affine_select(out=diag, in_=diag, compare_op=ALU.is_ge, fill=BIG, base=0,
                            pattern=[[0, 2], [-1, P]], channel_multiplier=1)
            for a in (1, 2):
                last = G.memset(va[a][:, :, :, HD:HD + 1], 1.0)
            last.then_inc(s_const, 1)
            pool.wait_ge(s_setup, N_SETUP)
            iterations(step, pool)


VALUES_AFTER = HG + 3
FILL_M2 = 5
NSTK = (None, 2 * len(TERMS_Q), 2 * len(TERMS_Q) + 1)
NEWTON = 3 + 3 * 3
N_WEIGHTS = 17
N_SETUP = 3 + 5 + 4 + 1 + TT * 2 * 4


def kernel(**inputs):
    import numpy as _np
    import concourse.bacc as _bacc
    from concourse import mybir as _mybir
    from concourse.bass_utils import run_bass_kernel_spmd as _run

    a = {k: _np.asarray(v) for k, v in inputs.items()}
    half = HD // 2
    freqs = _np.float32(32.0) ** (-_np.arange(0, HD, 2, dtype=_np.float32) / _np.float32(HD))
    angle = _np.arange(T, dtype=_np.float32)[:, None] * freqs[None, :].astype(_np.float32)

    def by_pairs(w):
        return w.reshape(D, HC, C, HD).transpose(0, 2, 3, 1).reshape(D, D)

    arrays = {
        "x": a["x"], "xT": a["x"].transpose(0, 2, 1), "ctxT": a["ctx_1024"].transpose(0, 2, 1),
        "mask": a["mask_BxS2_if1"],
        "wqk1": a["L0_attn_w_qkv"][:2 * D].T, "wv1": a["L0_attn_w_qkv"][2 * D:].T, "wo1": a["L0_attn_w_proj"].T,
        "wq2": by_pairs(a["L0_xattn_Wq"]), "wk2": by_pairs(a["L0_xattn_Wk"]), "wv2": a["L0_xattn_Wv"], "wo2": a["L0_xattn_Wo"],
        "w1h": a["L0_ffn_w1_h"].T, "w1l": a["L0_ffn_w1_l"].T, "w2h": a["L0_ffn_w2_h"].T, "w2l": a["L0_ffn_w2_l"].T,
        "b1h": a["L0_ffn_b1_h"].reshape(FCH - 1, P).T, "b1l": a["L0_ffn_b1_l"].reshape(1, P).T,
        "gam": _np.stack([a["L0_ffn_gamma_h"].reshape(C, P), a["L0_ffn_gamma_l"].reshape(C, P)]).transpose(2, 0, 1),
        "b2": _np.stack([a["L0_ffn_b2_h"], a["L0_ffn_b2_l"]]),
        "nw": _np.stack([a["L0_attn_q_norm_w"], a["L0_attn_k_norm_w"]]),
        "cossin": _np.concatenate([_np.cos(angle), _np.sin(angle)], axis=1).astype(_np.float32),
    }
    nc = _bacc.Bacc("TRN2", target_bir_lowering=False, num_devices=1)
    feed, io = {}, {}
    for name, value in arrays.items():
        value = _np.ascontiguousarray(value)
        feed[f"in_{name}"] = value
        io[name] = nc.dram_tensor(f"in_{name}", value.shape, _mybir.dt.from_np(value.dtype), kind="ExternalInput").ap()
    io["out"] = nc.dram_tensor("out_x", (B, T, D), _mybir.dt.float32, kind="ExternalOutput").ap()
    build(nc, io)
    r = _run(nc, [feed], core_ids=[0])
    return r.results[0]["out_x"]
```

```python
from contextlib import ExitStack

import numpy as np
import concourse.bass as bass
from concourse import mybir

B, T, D, H = 16, 256, 256, 16
HD = D // H
P = 128
TT = T // P
C = D // P
HC = P // HD
TERMS_Q = (0, 0, 0, 1, 1, 2)
TERMS_K = (0, 1, 2, 0, 1, 0)
NPROD = len(TERMS_Q) * HD
ROW_BIAS = NPROD
ROW_MAX = NPROD + 1
K_MAX = ROW_MAX
K_ALL = ROW_MAX + 3
VW = 32
HG = 4
NG = H // HG
FCH = 9
LIGHT = FCH - 1
BIG = -1e30
NORM_EPS, LN_EPS = 1e-6, 1e-5


def build(nc, io):
    f32, bf16, i32 = mybir.dt.float32, mybir.dt.bfloat16, mybir.dt.int32
    f32r = mybir.dt.float32r
    ALU, ACT, AX = mybir.AluOpType, mybir.ActivationFunctionType, mybir.AxisListType
    ctx = ExitStack()
    with ctx:
        def sb(name, shape, dt=f32):
            return ctx.enter_context(nc.sbuf_tensor(name, shape, dt))

        def sem(name):
            return ctx.enter_context(nc.semaphore(name))

        wqk1 = [sb(f"wqk1{part}", [P, C, 2 * D], f32r) for part in ("high", "low")]
        wv1 = [sb(f"wv1{part}", [P, C, D], f32r) for part in ("high", "low")]
        wo1 = sb("wo1", [P, C, D])
        wq2 = sb("wq2", [P, C, D]); wk2 = sb("wk2", [P, C, D]); wv2 = sb("wv2", [P, C, D])
        wo2 = sb("wo2", [P, C, D])
        w1h = sb("w1h", [P, C, FCH * P], f32r); w1l = sb("w1l", [P, C, FCH * P], f32r); w2 = sb("w2", [P, FCH, D])
        b1 = sb("b1", [P, FCH]); b2sum = sb("b2sum", [P, D])
        gam = sb("gam", [P, 2, C])
        cs = sb("cs", [P, TT, 2, HD // 2])
        nw = sb("nw", [P, 2, HD])
        ropeC = sb("ropeC", [P, TT, 2, HD]); ropeS = sb("ropeS", [P, TT, 2, HD])
        idf = sb("idf", [P, P]); idb = sb("idb", [P, P], bf16)
        cmask = sb("cmask", [P, 2, P])
        cmaskb = sb("cmaskb", [P, 2, P], bf16)
        maski = sb("maski", [B, T], i32); maskf = sb("maskf", [B, T]); maskb = sb("maskb", [B, T], bf16)
        xT = sb("xT", [P, C, T]); xTp = [sb(f"xT{part}", [P, C, T], f32r) for part in ("high", "low")]
        ctxT = sb("ctxT", [P, C, T]); x1T = sb("x1T", [P, C, T])
        xnh = sb("xnh", [P, C, T], f32r); xnl = sb("xnl", [P, C, T], f32r)
        x0 = sb("x0", [P, TT, D]); x1c = sb("x1c", [P, TT, D])
        y = [None, sb("y1", [P, TT, D]), sb("y2", [P, TT, D]), sb("y3", [P, TT, D])]
        st = [None] + [sb(f"st{a}", [P, TT, 6]) for a in (1, 2, 3)]
        mv = [None] + [sb(f"mv{a}", [P, TT, 2]) for a in (1, 2, 3)]
        rstd = [None] + [sb(f"rstd{a}", [P, TT]) for a in (1, 2, 3)]
        ve = [None] + [sb(f"ve{a}", [P, TT]) for a in (1, 2, 3)]
        xo = [None, sb("x1", [P, TT, D]), sb("x2", [P, TT, D]), sb("x3", [P, TT, D])]
        sq = sb("sq", [P, TT, 2 * D]); ss = sb("ss", [P, TT, 2 * H]); rr = sb("rr", [P, TT, 2 * H]); ms = sb("ms", [P, TT, 2 * H]); nt = sb("nt", [P, TT, 2 * H])
        qn = sb("qn", [P, TT, 2 * D]); rot = sb("rot", [P, TT, 2 * D]); qc = sb("qc", [P, TT, 2 * D]); qr = sb("qr", [P, TT, 2 * D])
        sq2 = sb("sq2", [P, TT, D]); ss2 = sb("ss2", [P, TT]); xn = sb("xn", [P, TT, D])
        x2b = sb("x2b", [P, TT, D]); rr2 = sb("rr2", [P, TT]); ssm = sb("ssm", [P, TT])
        warm = sb("warm", [P, 1])
        minus_half = sb("minus_half", [P, TT])
        nat = [None] + [[sb(f"nat{a}{s}", [P, 3, C * T], bf16) for s in "qk"] for a in (1, 2)]
        rest = sb("rest", [P, C * T])
        stk = [None] + [[sb(f"stk{a}{s}", [K_ALL, H, T], bf16) for s in "qk"] for a in (1, 2)]
        va = [None] + [sb(f"va{a}", [P, TT, H, VW]) for a in (1, 2)]
        mx3 = sb("mx3", [P, H, 3])
        mx2 = sb("mx2", [P, TT, H])
        nm = [None] + [sb(f"nm{a}", [P, TT, H]) for a in (1, 2)]
        nr = [None] + [sb(f"nr{a}", [P, TT, H]) for a in (1, 2)]
        mp = [None] + [sb(f"mp{a}", [P, TT, 3, H], bf16) for a in (1, 2)]
        mT = [None] + [sb(f"mT{a}", [3 * H, T], bf16) for a in (1, 2)]
        pr = sb("pr", [P, 2 * HG, 3 * P])
        oT = [None] + [sb(f"oT{a}", [P, NG, T]) for a in (1, 2)]
        rden = [None] + [sb(f"rden{a}", [P, TT, H]) for a in (1, 2)]
        on = [None] + [sb(f"on{a}", [P, TT, D]) for a in (1, 2)]
        onT = [None] + [sb(f"onT{a}", [P, C, T]) for a in (1, 2)]
        g = sb("g", [P, FCH, T])
        b2 = y[3]
        staged = pr[:, :, :].rearrange("p h t -> p (h t)")
        wqk1raw = staged[:, 0:2 * C * D].rearrange("p (c n) -> p c n", c=C)
        wv1raw = staged[:, 2 * C * D:3 * C * D].rearrange("p (c n) -> p c n", c=C)
        w1raw = g[:, :, :].rearrange("p j t -> p (j t)").rearrange("p (c n) -> p c n", c=C)
        kb = nc.dram_tensor("kb", [B, T], bf16)

        bank = [ctx.enter_context(nc.psum_tensor(f"bank{i}", [P, 512], f32)) for i in range(8)]
        bankb = [bk[:, :].bitcast(bf16) for bk in bank]
        FFN_BANK, OT_BANK = 7, 6
        MAX_BANK, TOK_BANK, DIM_BANK, PROJ_BANK = (None, 0, 2), 2, 2, 3
        V_BANK = (None, 1, 4)
        S_BANKS, ST_BANKS = (0, 1, 6), (2, 3, 0)
        SPLIT_BANK = (None, (4, 5), (6, 5))

        def two(name):
            return [None, sem(name + "1"), sem(name + "2")]

        s_xhigh = sem("xT_high_ready"); s_xlow = sem("xT_low_ready"); s_whalf = sem("self_weights_halved")
        s_wqk1 = sem("wqk1_loaded"); s_wself = sem("self_weights_loaded"); s_wcross = sem("cross_weights_loaded"); s_wffn = sem("ffn_weights_loaded")
        s_const = sem("consts_ready"); s_mask = sem("keybias_step"); s_rows = sem("fixed_rows_ready")
        s_table = sem("rope_table_step"); s_scaled = sem("ffn_weights_scaled"); s_halved = sem("w1_high_ready"); s_w1 = sem("w1_halves_ready"); s_xnhigh = sem("xn_high_ready")
        s_kb = sem("keybias_stored"); s_pool = sem("pool_step")
        s_xT = sem("xT_loaded"); s_ctxT = sem("ctxT_loaded"); s_x0 = sem("x0_loaded")
        s_qk1 = sem("qk1_ready"); s_sq = sem("squares_ready"); s_ss = sem("dve_ss");
        s_qn = sem("qn_ready"); s_rot = sem("pool_rot"); s_rope = sem("rope_ready")
        s_v = two("v_ready"); s_va = two("va_ready")
        s_nat = two("nat_ready"); s_hi = two("hi_ready"); s_rest = two("dve_rest"); s_mid = two("dve_mid")
        s_split = two("split_ready"); s_stk = two("stack_loaded")
        s_s = two("scores_ready"); s_mx = two("max_ready"); s_nm = two("dve_nm"); s_mp = two("maxparts_ready")
        s_mt = two("maxT_ready"); s_mT = two("maxT_copied"); s_ml = two("max_loaded")
        s_st = two("scoresT_ready"); s_exp = two("exp_ready"); s_prob = two("probs_ready")
        s_pv = two("out_ready"); s_oT = two("outT_copied"); s_ott = two("outtok_ready")
        s_rd = two("dve_rden"); s_on = two("on_ready"); s_ont = two("onT_ready"); s_onT = two("onT_copied")
        s_o = [None, sem("proj1_ready"), sem("proj2_ready"), sem("ffn_ready")]
        s_y = [None] + [sem(f"dve_y{a}") for a in (1, 2, 3)]
        s_bn = [None] + [sem(f"dve_bn{a}") for a in (1, 2, 3)]
        s_mv = [None] + [sem(f"dve_mv{a}") for a in (1, 2, 3)]
        s_rs = [None] + [sem(f"dve_rs{a}") for a in (1, 2, 3)]
        s_ve = [None] + [sem(f"var{a}_ready") for a in (1, 2, 3)]
        s_x = [None] + [sem(f"x{a}_ready") for a in (1, 2, 3)]
        s_x1t = sem("x1T_ready"); s_x1T = sem("x1T_copied")
        s_ss2 = sem("ss2_ready"); s_sc2 = sem("scale2_ready"); s_ssm = sem("ssm_ready"); s_xn = sem("xn_ready")
        s_xnt = sem("xnT_ready"); s_xnT = sem("xnT_low_ready"); s_x2b = sem("x2b_ready"); s_x1c = sem("x1c_ready"); s_new = sem("dve_newton")
        s_h = sem("hidden_ready"); s_g = sem("gelu_ready"); s_out = sem("out_stored"); s_warm = sem("exp_table_loaded")

        def wait(eng, s, value):
            if isinstance(value, int) and value <= 0:
                return
            eng.wait_ge(s, value)

        def wait_apart(eng, *waits):
            waits = [(s, v if isinstance(v, int) else eng.to_reg(v)) for s, v in waits]
            eng.wait_ge(s_const, 1)
            for s, value in waits:
                wait(eng, s, value)

        def tokens(dram, b):
            return dram[bass.ds(b, 1)].rearrange("o (t p) d -> p (o t) d", p=P)

        def dims(dram, b):
            return dram[bass.ds(b, 1)].rearrange("o (c p) t -> p (o c) t", p=P)

        def first(b):
            return isinstance(b, int) and b == 0

        def starting(b):
            return isinstance(b, int) and 0 <= b < 2

        def live(b):
            return not isinstance(b, int) or 0 <= b < B

        def iterations(step, eng):
            for i in range(-1, 4):
                step(i)
            with eng.Fori(4, B - 2) as i:
                step(i)
            for i in range(B - 2, B + 3):
                step(i)

        h2 = HD // 2

        def rotate(eng, ops, b):
            for t in range(TT):
                n = TT * b + t
                eng.wait_ge(s_qn, n + 1)
                wait(eng, s_nat[1], 2 * b)
                four = "p (s h f d) -> p s h f d"
                qv = qn[:, t, :].rearrange(four, s=2, h=H, f=2)
                rv = rot[:, t, :].rearrange(four, s=2, h=H, f=2)
                for s in range(2):
                    ops.tensor_tensor(qc[:, t, s * D:(s + 1) * D].rearrange("p (h d) -> p h d", d=HD),
                                    qn[:, t, s * D:(s + 1) * D].rearrange("p (h d) -> p h d", d=HD),
                                    ropeC[:, t, s:s + 1, :].to_broadcast([P, H, HD]), ALU.mult)
                    for half in range(2):
                        last = ops.tensor_tensor(rv[:, s, :, half, :], qv[:, s, :, 1 - half, :],
                                               ropeS[:, t, s:s + 1, half * h2:(half + 1) * h2]
                                               .to_broadcast([P, H, h2]), ALU.mult)
                last.then_inc(s_rot, 1)
                eng.wait_ge(s_rot, n + 1)
                for s in range(2):
                    pairs = "p (j c d) -> p j c d"
                    last = ops.tensor_tensor(qr[:, t, s * D:(s + 1) * D].rearrange("p (c d j) -> p j c d", c=C, d=HD),
                                           qc[:, t, s * D:(s + 1) * D].rearrange(pairs, c=C, d=HD),
                                           rot[:, t, s * D:(s + 1) * D].rearrange(pairs, c=C, d=HD), ALU.add)
                last.then_inc(s_rope, 1)

        block = ctx.enter_context(nc.Block())

        @block.sync
        def _(sp):
            def load(dst, src, s):
                sp.dma_start(dst, src).then_inc(s, 16)

            load(xT[:, :, :], dims(io["xT"], 0), s_xT)
            load(wqk1raw, io["wqk1"].rearrange("(c p) n -> p c n", p=P), s_wqk1)
            load(cs[:, :, :, :], io["cossin"].rearrange("(t p) (s d) -> p t s d", p=P, s=2), s_wself)
            load(nw[:, :, :], io["nw"].rearrange("(o s) d -> o s d", o=1).to_broadcast([P, 2, HD]), s_wself)
            load(maski[:, :], io["mask"], s_kb)
            load(wv1raw, io["wv1"].rearrange("(c p) n -> p c n", p=P), s_wself)
            sp.wait_ge(s_mask, 3)
            load(kb.ap(), maskb[:, :], s_kb)
            sp.wait_ge(s_kb, 32)

            def stacks(a, b):
                wait_apart(sp, (s_pv[a], NG * b))
                if a == 2 and first(b):
                    sp.wait_ge(s_rows, 5)
                if a == 2:
                    load(stk[2][1][ROW_BIAS:ROW_BIAS + 1, :, :],
                         kb.ap()[bass.ds(b, 1), :].rearrange("o (h t) -> o h t", h=1).to_broadcast([1, H, T]), s_stk[2])
                for nth, s in enumerate((None, (0, 1), (1, 0))[a]):
                    wait_apart(sp, (s_split[a], 2 * b + nth + 1))
                    for r, part in enumerate((TERMS_Q, TERMS_K)[s]):
                        load(stk[a][s][r * HD:(r + 1) * HD, :, :], nat[a][s][:, part, :], s_stk[a])

            def maxima(a, b):
                wait_apart(sp, (s_mT[a], b + 1))
                load(stk[a][0][ROW_MAX:ROW_MAX + 3, :, :], mT[a][:, :], s_ml[a])

            def step(i):
                if live(i):
                    wait_apart(sp, (s_y[1], i))
                    load(x0[:, :, :], tokens(io["x"], i), s_x0)
                    maxima(1, i)
                if live(i - 1):
                    stacks(2, i - 1)
                if live(i):
                    wait_apart(sp, (s_v[2], i))
                    load(ctxT[:, :, :], dims(io["ctxT"], i), s_ctxT)
                if live(i - 1):
                    maxima(2, i - 1)
                if live(i + 1):
                    stacks(1, i + 1)
                if live(i + 2):
                    wait_apart(sp, (s_xlow, i + 2))
                    load(xT[:, :, :], dims(io["xT"], i + 2), s_xT)
                if live(i - 3):
                    wait_apart(sp, (s_x[3], TT * (i - 2)))
                    load(tokens(io["out"], i - 3), xo[3][:, :, :], s_out)

            iterations(step, sp)
            sp.wait_ge(s_out, 16 * B)

        @block.tensor
        def _(pe):
            def mm(out, lhsT, rhs, start, stop, check=False):
                return nc.tensor.matmul(out, lhsT, rhs, start=start, stop=stop, skip_group_check=check)

            def tok_proj(out, src, t, w, lo, n):
                for c in range(C):
                    last = mm(out, src[:, c, t * P:(t + 1) * P], w[:, c, lo:lo + n], c == 0, c == C - 1)
                return last

            def halves_proj(out, src, t, w):
                products = [(x, y, c) for x, y in ((src[0], w[0]), (src[0], w[1]), (src[1], w[0])) for c in range(C)]
                for n, (x, y, c) in enumerate(products):
                    last = mm(out, x[:, c, t * P:(t + 1) * P], y[:, c, :], n == 0, n == len(products) - 1)
                return last

            def dim_proj(out, w, lo, src):
                for c in range(C):
                    last = mm(out, w[:, c, lo:lo + P], src[:, c, :], c == 0, c == C - 1)
                return last

            def four_transposes(k, src):
                for c in range(C):
                    for t in range(TT):
                        last = nc.tensor.transpose(bank[k][:, c * T + t * P:c * T + (t + 1) * P],
                                                   src[:, t, c * P:(c + 1) * P], idf[:, :])
                return last

            def qk1(b, t):
                if t == 0:
                    pe.wait_ge(s_xlow, b + 1)
                    if live(b - 1):
                        pe.wait_ge(s_mx[1], H * (b - 1) + 14)
                else:
                    wait(pe, s_va[2], b - 1)
                halves_proj(bank[(1, 4)[t]][:, :], xTp, t, wqk1).then_inc(s_qk1, 1)

            def v1(b):
                if first(b):
                    pe.wait_ge(s_whalf, 4)
                wait(pe, s_mx[2], H * (b - 2) + 14 if live(b - 2) else 0)
                for t in range(TT):
                    last = halves_proj(bank[V_BANK[1]][:, t * D:(t + 1) * D], xTp, t, wv1)
                last.then_inc(s_v[1], 1)

            def transpose_x1(b):
                pe.wait_ge(s_x[1], TT * (b + 1))
                if live(b + 1):
                    pe.wait_ge(s_mx[1], H * (b + 2))
                four_transposes(6, xo[1]).then_inc(s_x1t, 1)

            def k2(b):
                if live(b + 1):
                    pe.wait_ge(s_rest[1], 2 * (b + 2))
                for c in range(C):
                    last = dim_proj(bank[5][:, c * T:(c + 1) * T], wk2, c * P, ctxT)
                last.then_inc(s_nat[2], 1)

            def v2(b):
                if first(b):
                    pe.wait_ge(s_wcross, 16 * N_CROSS)
                pe.wait_ge(s_ctxT, 16 * (b + 1))
                if live(b + 1):
                    pe.wait_ge(s_rest[1], 2 * (b + 1) + 1)
                for t in range(TT):
                    last = tok_proj(bank[V_BANK[2]][:, t * D:(t + 1) * D], ctxT, t, wv2, 0, D)
                last.then_inc(s_v[2], 1)

            def q2(b):
                pe.wait_ge(s_x1T, b + 1)
                for c in range(C):
                    last = dim_proj(bank[6][:, c * T:(c + 1) * T], wq2, c * P, x1T)
                last.then_inc(s_nat[2], 1)

            def transpose_xn(b):
                pe.wait_ge(s_xn, TT * (b + 1))
                if live(b + 1):
                    pe.wait_ge(s_rest[2], 2 * (b + 1) + 1)
                four_transposes(5, xn).then_inc(s_xnt, 1)

            def hidden(b, j):
                k = 4 + j % 2
                if j == 0:
                    if first(b):
                        pe.wait_ge(s_w1, 1)
                    pe.wait_ge(s_xnT, b + 1)
                    if live(b + 3):
                        pe.wait_ge(s_qn, TT * (b + 4))
                elif j >= 2:
                    pe.wait_ge(s_g, FCH * b + j - 1)
                products = [(w, x, c) for w, x in ((w1h, xnh), (w1h, xnl), (w1l, xnh)) for c in range(C)]
                for n, (w, x, c) in enumerate(products):
                    last = mm(bank[k][:, 0:T], w[:, c, j * P:(j + 1) * P], x[:, c, :], n == 0, n == len(products) - 1)
                last.then_inc(s_h, 1)

            def transpose_qk1(b):
                pe.wait_ge(s_rope, TT * (b + 1))
                wait(pe, s_g, FCH * (b - 2))
                for s in range(2):
                    four_transposes(4 + s, qr[:, :, s * D:(s + 1) * D]).then_inc(s_nat[1], 1)

            def scores(a, b, h):
                if h == 0:
                    if first(b):
                        pe.wait_ge(s_rows, (None, 3, 5)[a])
                    pe.wait_ge(s_stk[a], 16 * NSTK[a] * (b + 1))
                    if live((b - 2, b + 1)[a - 1]):
                        pe.wait_ge(s_exp[3 - a], H * (b - 2, b + 1)[a - 1] + 15)
                if h == 1 and a == 1:
                    pe.wait_ge(s_va[1], b + 1)
                if h == 1 and a == 2 and live(b + 2):
                    pe.wait_ge(s_qn, TT * (b + 2) + 1)
                if h == 2 and live((b - 2, b + 1)[a - 1]):
                    pe.wait_ge(s_oT[3 - a], NG * (b - 1, b + 2)[a - 1])
                if h >= 3:
                    pe.wait_ge(s_mx[a], H * b + h - 2)
                k = S_BANKS[h % 3]
                q, kk = stk[a]
                on_pe = a == MASKED_ON_PE
                if on_pe:
                    blocks = bank[k][:, 0:3 * P].rearrange("p (k t) -> p k t", k=3)
                    mm(blocks[:, 0:3:2, :], idb[:, :], cmaskb[:, :, :], True, False, True)
                mm(bank[k][:, 0:P], q[0:K_MAX, h, 0:P], kk[0:K_MAX, h, 0:P], not on_pe, not on_pe, True)
                mm(bank[k][:, P:3 * P], q[0:K_MAX, h, P:T], kk[0:K_MAX, h, :], not on_pe, True, True)\
                    .then_inc(s_s[a], 1)

            def transpose_max(a, b):
                wait_apart(pe, (s_mp[a], b + 1))
                for t in range(TT):
                    last = nc.tensor.transpose(bankb[MAX_BANK[a]][0:3 * H, t * P:(t + 1) * P], mp[a][:, t, :, :], idb[:, :])
                last.then_inc(s_mt[a], 1)

            def scores_t(a, b, h):
                if h == 0:
                    pe.wait_ge(s_ml[a], 16 * (b + 1))
                if h == 1:
                    if a == 2 and live(b + 1):
                        pe.wait_ge(s_y[1], b + 2)
                    if a == 1:
                        wait(pe, s_y[2], b - 1)
                k = ST_BANKS[h % 3]
                if h >= 3:
                    pe.wait_ge(s_exp[a], H * b + h - 2)
                q, kk = stk[a]
                mm(bank[k][:, 0:T], kk[0:K_ALL, h, 0:P], q[0:K_ALL, h, :], True, True)
                mm(bank[k][:, T:3 * P], kk[0:K_ALL, h, P:T], q[0:K_ALL, h, P:T], True, True).then_inc(s_st[a], 1)

            def values(a, b, gr):
                pe.wait_ge(s_prob[a], H * b + HG * (gr + 1))
                if gr == 0 and a == 1:
                    wait(pe, s_rest[2], 2 * b)
                if gr > 0:
                    pe.wait_ge(s_oT[a], NG * b + gr)
                for key in range(2):
                    for j in range(HG):
                        h = HG * gr + j
                        out = bank[OT_BANK][VW * j:VW * (j + 1), :]
                        if key == 0:
                            mm(out[:, 0:T], va[a][:, 0, h, :], pr[:, h % (2 * HG), 0:T], True, False, True)
                        else:
                            last = mm(out[:, P:T], va[a][:, 1, h, :], pr[:, h % (2 * HG), T:3 * P], False, True, True)
                last.then_inc(s_pv[a], 1)

            def out_tokens(a, b):
                pe.wait_ge(s_oT[a], NG * (b + 1))
                for t in range(TT):
                    for gr in range(NG):
                        last = nc.tensor.transpose(bank[TOK_BANK + t][:, gr * P:(gr + 1) * P],
                                                   oT[a][:, gr, t * P:(t + 1) * P], idf[:, :])
                    last.then_inc(s_ott[a], 1)

            def out_dims(a, b):
                pe.wait_ge(s_on[a], TT * (b + 1))
                four_transposes(DIM_BANK, on[a]).then_inc(s_ont[a], 1)

            def out_proj(a, b):
                if first(b):
                    pe.wait_ge(s_wcross, 16 * N_CROSS)
                pe.wait_ge(s_onT[a], b + 1)
                for t in range(TT):
                    last = tok_proj(bank[PROJ_BANK][:, t * D:(t + 1) * D], onT[a], t, (None, wo1, wo2)[a], 0, D)
                last.then_inc(s_o[a], 1)

            def ffn_out(b, t, j):
                if t == 0 and j == 0:
                    wait(pe, s_y[3], b)
                if t == 0:
                    pe.wait_ge(s_g, FCH * b + j + 1)
                last = mm(bank[FFN_BANK][:, t * D:(t + 1) * D], g[:, j, t * P:(t + 1) * P], w2[:, j, :],
                          j == 0, j == FCH - 1)
                if t == TT - 1 and j == FCH - 1:
                    last.then_inc(s_o[3], 1)

            def phase(heads, others):
                for h in range(H + 1):
                    for other in others.get(h, []):
                        other()
                    if heads and h < H:
                        heads(h)

            def step(i):
                s, c, f, l = i, i - 1, i - 2, i - 3
                others = {}

                def add(at, fn, *args):
                    others.setdefault(at, []).append(lambda: fn(*args))

                if live(f):
                    add(OUT2_AT[0], values, 2, f, NG - 1)
                    add(OUT2_AT[1], out_tokens, 2, f)
                    add(OUT2_AT[2], out_dims, 2, f)
                    add(OUT2_AT[3], out_proj, 2, f)
                if live(c):
                    add(K2_AT, k2, c)
                phase((lambda h: scores(1, s, h)) if live(s) else None, others)
                if live(i + 1):
                    qk1(i + 1, 0)
                if live(s):
                    transpose_max(1, s)
                if live(c):
                    transpose_x1(c)
                if live(i + 1):
                    qk1(i + 1, 1)
                if live(c):
                    q2(c)
                others = {}
                if live(l):
                    for j in range(FCH):
                        add(FFN_C[j], ffn_out, l, 1, j)
                if live(f):
                    add(XN_AT, transpose_xn, f)
                if live(s):
                    for gr in range(NG - 1):
                        add(HG * gr + VALUES_AFTER, values, 1, s, gr)
                phase((lambda h: scores_t(1, s, h)) if live(s) else None, others)
                others = {}
                if live(s):
                    add(OUT1_AT[0], values, 1, s, NG - 1)
                    add(OUT1_AT[1], out_tokens, 1, s)
                    add(OUT1_AT[2], out_dims, 1, s)
                    add(OUT1_AT[3], out_proj, 1, s)
                if live(f):
                    for j in range(FCH):
                        add(HIDDEN_D[j], hidden, f, j)
                phase((lambda h: scores(2, c, h)) if live(c) else None, others)
                if live(i + 1):
                    transpose_qk1(i + 1)
                    v1(i + 1)
                if live(c):
                    transpose_max(2, c)
                others = {}
                if live(f):
                    for j in range(FCH):
                        add(FFN_F[j], ffn_out, f, 0, j)
                if live(s):
                    add(V2_AT, v2, s)
                if live(c):
                    for gr in range(NG - 1):
                        add(HG * gr + VALUES_AFTER, values, 2, c, gr)
                phase((lambda h: scores_t(2, c, h)) if live(c) else None, others)

            pe.wait_ge(s_whalf, 2)
            pe.wait_ge(s_const, 1)
            iterations(step, pe)

        @block.scalar
        def _(act):
            def copy(out, in_):
                return nc.scalar.activation(out, in_, ACT.Copy)

            def copy_v(a, b):
                act.wait_ge(s_v[a], b + 1)
                wait(act, s_pv[a], NG * b)
                copy(va[a][:, :, :, 0:HD], bank[V_BANK[a]][:, :].rearrange("p (t h d) -> p t h d", t=TT, h=H))\
                    .then_inc(s_va[a], 1)

            def copy_dims(dst, k):
                return copy(dst[:, :, :], bank[k][:, :].rearrange("p (c t) -> p c t", c=C))

            def copy_out(a, b):
                act.wait_ge(s_ont[a], b + 1)
                copy_dims(onT[a], DIM_BANK).then_inc(s_onT[a], 1)

            def copy_group(a, b, gr):
                act.wait_ge(s_pv[a], NG * b + gr + 1)
                wait(act, s_ott[a], TT * b)
                copy(oT[a][:, gr, :], bank[OT_BANK][:, 0:T]).then_inc(s_oT[a], 1)

            def exponentials(a, b, h):
                if h % HG == 0 and h >= 2 * HG:
                    copy_group(a, b, h // HG - 2)
                act.wait_ge(s_st[a], H * b + h + 1)
                if h >= 2 * HG:
                    act.wait_ge(s_pv[a], NG * b + h // HG - 1)
                else:
                    if a == 1:
                        wait(act, s_pv[2], NG * (b - 1) - 1 + h // HG)
                    elif live(b + 1):
                        act.wait_ge(s_pv[1], NG * (b + 2) - 1 + h // HG)
                    else:
                        act.wait_ge(s_pv[2], NG * b - 1 + h // HG)
                nc.scalar.activation(pr[:, h % (2 * HG), :], bank[ST_BANKS[h % 3]][:, 0:3 * P], ACT.Exp, scale=HD ** -0.5)\
                    .then_inc(s_exp[a], 1)
                if h == H - 1:
                    copy_group(a, b, NG - 2)
                    copy_group(a, b, NG - 1)

            def load_ffn():
                load(w1raw[:, :, 0:LIGHT * P], io["w1h"].rearrange(chunks, p=P), s_wffn)
                load(w1raw[:, :, LIGHT * P:FCH * P], io["w1l"].rearrange(chunks, p=P), s_wffn)
                load(w2[:, 0:LIGHT, :], io["w2h"].rearrange(chunks, p=P), s_wffn)
                load(w2[:, LIGHT, :], io["w2l"], s_wffn)
                load(b1[:, 0:LIGHT], io["b1h"], s_wffn)
                load(b1[:, LIGHT:FCH], io["b1l"], s_wffn)
                load(gam[:, :, :], io["gam"], s_wffn)
                load(b2[:, :, :], io["b2"].rearrange("(o s) d -> o s d", o=1).to_broadcast([P, 2, D]), s_wffn)

            def step(i):
                s, c, f = i, i - 1, i - 2
                if live(i + 1):
                    act.wait_ge(s_xT, 16 * (i + 2))
                    wait(act, s_v[1], i + 1)
                    copy(xTp[0][:, :, :], xT[:, :, :]).then_inc(s_xhigh, 1)
                if live(c):
                    copy_v(2, c)
                if live(f):
                    copy_out(2, f)
                if live(c):
                    act.wait_ge(s_x1t, c + 1)
                    wait(act, s_nat[2], 2 * c)
                    copy_dims(x1T, 6).then_inc(s_x1T, 1)
                if live(c):
                    high_part(2, c, 1, 0)
                if live(i + 1):
                    squares(i + 1, 0)
                if live(i + 1):
                    squares(i + 1, 1)
                if live(f):
                    norms(f)
                if live(c):
                    high_part(2, c, 0, 1)
                for h in range(H):
                    if h == XNT_AT and live(f):
                        act.wait_ge(s_xnt, f + 1)
                        wait(act, s_h, FCH * f)
                        copy_dims(xnh, 5).then_inc(s_xnhigh, 1)
                    if live(s):
                        exponentials(1, s, h)
                if first(i):
                    load_ffn()
                for j in range(FCH):
                    if live(f):
                        act.wait_ge(s_h, FCH * f + j + 1)
                        if j == 0:
                            if first(f):
                                act.wait_ge(s_wffn, 16 * N_FFN)
                                act.wait_ge(s_w1, 1)
                            wait(act, s_o[3], f)
                        nc.scalar.activation(g[:, j, :], bank[4 + j % 2][:, 0:T], ACT.Gelu, bias=b1[:, j:j + 1])\
                            .then_inc(s_g, 1)
                    if j == COPY1_AT and live(s):
                        copy_out(1, s)
                wait(act, s_warm, i + 1)
                nc.scalar.activation(warm[:, :], minus_half[:, 0:1], ACT.Exp).then_inc(s_warm, 1)
                if live(i + 1):
                    high_part(1, i + 1, 0, 0)
                    high_part(1, i + 1, 1, 1)
                    copy_v(1, i + 1)
                if live(c):
                    for h in range(H):
                        exponentials(2, c, h)

            def squares(b, t):
                act.wait_ge(s_qk1, TT * b + t + 1)
                wait(act, s_ss, TT * b)
                nc.scalar.activation(sq[:, t, :], bank[(1, 4)[t]][:, :], ACT.Square).then_inc(s_sq, 1)

            def norms(b):
                wait(act, s_ssm, b)
                for t in range(TT):
                    act.wait_ge(s_x[2], TT * b + t + 1)
                    nc.scalar.activation(sq2[:, t, :], xo[2][:, t, :], ACT.Square,
                                         accum_out=ss2[:, t:t + 1]).then_inc(s_ss2, 1)

            def high_part(a, b, s, nth):
                act.wait_ge(s_nat[a], 2 * b + nth + 1)
                wait(act, s_stk[a], 16 * NSTK[a] * b)
                copy(nat[a][s][:, 0, :], bank[SPLIT_BANK[a][s]][:, :]).then_inc(s_hi[a], 1)

            def load(dst, src, s):
                act.dma_start(dst, src).then_inc(s, 16)

            chunks = "(c p) n -> p c n"
            for w, name in ((wo1, "wo1"), (wk2, "wk2"), (wv2, "wv2"), (wq2, "wq2"), (wo2, "wo2")):
                load(w[:, :, :], io[name].rearrange(chunks, p=P), s_wcross)
            act.wait_ge(s_const, 1)
            iterations(step, act)

        @block.vector
        def _(dve):
            V = nc.vector

            def split(a, b, s, nth):
                dve.wait_ge(s_hi[a], 2 * b + nth + 1)
                n = nat[a][s]
                if nth == 1:
                    dve.wait_ge(s_split[a], 2 * b + 1)
                elif a == 2:
                    dve.wait_ge(s_split[1], 2 * (b + 2) if live(b + 1) else 2 * B)
                else:
                    wait(dve, s_split[2], 2 * (b - 1))
                V.tensor_tensor(rest[:, :], bank[SPLIT_BANK[a][s]][:, :], n[:, 0, :], ALU.subtract)\
                    .then_inc(s_rest[a], 1)
                dve.wait_ge(s_rest[a], 2 * b + nth + 1)
                V.tensor_copy(n[:, 1, :], rest[:, :]).then_inc(s_mid[a], 1)
                dve.wait_ge(s_mid[a], 2 * b + nth + 1)
                V.tensor_tensor(n[:, 2, :], rest[:, :], n[:, 1, :], ALU.subtract).then_inc(s_split[a], 1)

            cm = cmask[:, :, :].rearrange("p k t -> p (k t)")

            def maxima(a, b, between):
                for h in range(H):
                    if h in between:
                        between[h]()
                    if a == MASKED_ON_PE:
                        dve.wait_ge(s_s[a], H * b + h + 1)
                        V.tensor_reduce(mx3[:, h, :], bank[S_BANKS[h % 3]][:, 0:3 * P].rearrange("p (k t) -> p k t", k=3),
                                        AX.X, ALU.max, negate=True).then_inc(s_mx[a], 1)
                        continue
                    wait_apart(dve, (s_s[a], H * b + h + 1))
                    for t, lo, hi in ((0, 0, P), (1, P, 3 * P)):
                        masked = bank[S_BANKS[h % 3]][:, lo:hi]
                        last = V.tensor_tensor_reduce(out=masked, in0=masked, in1=cm[:, 2 * P - (hi - lo):2 * P],
                                                      scale=1.0, scalar=-3e38, op0=ALU.add, op1=ALU.max,
                                                      accum_out=mx2[:, t, h:h + 1])
                    last.then_inc(s_mx[a], 1)
                dve.wait_ge(s_mx[a], H * (b + 1))
                if a == MASKED_ON_PE:
                    V.tensor_copy(nm[a][:, 0, :], mx3[:, :, 0])
                    V.tensor_tensor(nm[a][:, 1, :], mx3[:, :, 1], mx3[:, :, 2], ALU.min).then_inc(s_nm[a], 1)
                else:
                    V.tensor_scalar(nm[a][:, :, :], mx2[:, :, :], -1.0, None, ALU.mult).then_inc(s_nm[a], 1)
                dve.wait_ge(s_nm[a], 4 * b + 1)
                wait(dve, s_mt[a], b)
                V.tensor_copy(mp[a][:, :, 0, :], nm[a][:, :, :]).then_inc(s_nm[a], 1)
                dve.wait_ge(s_nm[a], 4 * b + 2)
                V.tensor_tensor(nr[a][:, :, :], nm[a][:, :, :], mp[a][:, :, 0, :], ALU.subtract).then_inc(s_nm[a], 1)
                dve.wait_ge(s_nm[a], 4 * b + 3)
                V.tensor_copy(mp[a][:, :, 1, :], nr[a][:, :, :]).then_inc(s_nm[a], 1)
                dve.wait_ge(s_nm[a], 4 * b + 4)
                V.tensor_tensor(mp[a][:, :, 2, :], nr[a][:, :, :], mp[a][:, :, 1, :], ALU.subtract).then_inc(s_mp[a], 1)

            def max_t(a, b):
                dve.wait_ge(s_mt[a], b + 1)
                wait(dve, s_ml[a], 16 * b)
                V.tensor_copy(mT[a][:, :], bankb[MAX_BANK[a]][0:3 * H, 0:T]).then_inc(s_mT[a], 1)

            def normalise_heads(a, b):
                for t in range(TT):
                    dve.wait_ge(s_ott[a], TT * b + t + 1)
                    o = bank[TOK_BANK + t][:, :].rearrange("p (h w) -> p h w", w=VW)
                    V.reciprocal(rden[a][:, t, :], o[:, :, HD]).then_inc(s_rd[a], 1)
                    dve.wait_ge(s_rd[a], TT * b + t + 1)
                    wait(dve, s_ont[a], b)
                    V.tensor_tensor(on[a][:, t, :].rearrange("p (h d) -> p h d", d=HD), o[:, :, 0:HD],
                                    rden[a][:, t, :].rearrange("p (h o) -> p h o", o=1).to_broadcast([P, H, HD]),
                                    ALU.mult).then_inc(s_on[a], 1)

            def add_residual(a, b, k, resid):
                dve.wait_ge(s_o[a], b + 1)
                wait(dve, s_x[a], TT * b)
                V.tensor_tensor(y[a][:, :, :], bank[k][:, :].rearrange("p (t d) -> p t d", t=TT), resid[:, :, :], ALU.add)\
                    .then_inc(s_y[a], 1)

            def layer_norm(a, b):
                dve.wait_ge(s_y[a], b + 1)
                for t in range(TT):
                    V.bn_stats(st[a][:, t, :], y[a][:, t, :]).then_inc(s_bn[a], 1)
                for t in range(TT):
                    wait_apart(dve, (s_bn[a], TT * b + t + 1))
                    V.bn_aggr(mv[a][:, t, :], st[a][:, t, :]).then_inc(s_mv[a], 1)
                dve.wait_ge(s_mv[a], TT * (b + 1))
                wait(dve, s_rs[a], b)
                V.tensor_scalar(ve[a][:, :], mv[a][:, :, 1], LN_EPS, None, ALU.add).then_inc(s_ve[a], 1)
                dve.wait_ge(s_rs[a], b + 1)
                if a == 1:
                    wait(dve, s_x1t, b)
                    wait(dve, s_x1c, b)
                elif a == 2:
                    wait(dve, s_x2b, b)
                else:
                    wait(dve, s_out, 16 * b)
                for t in range(TT):
                    V.tensor_scalar(xo[a][:, t, :], y[a][:, t, :], mv[a][:, t, 0:1], rstd[a][:, t:t + 1],
                                    ALU.subtract, ALU.mult).then_inc(s_x[a], 1)

            def clamp2(b):
                dve.wait_ge(s_ss2, TT * (b + 1))
                wait(dve, s_sc2, b)
                V.tensor_scalar(ssm[:, :], ss2[:, :], 1e-24, None, ALU.max).then_inc(s_ssm, 1)

            def scale2(b):
                dve.wait_ge(s_sc2, b + 1)
                wait(dve, s_xnt, b)
                for t in range(TT):
                    V.tensor_scalar(xn[:, t, :], xo[2][:, t, :], rr2[:, t:t + 1], None, ALU.mult).then_inc(s_xn, 1)

            def scaled_qk(b):
                for t in range(TT):
                    dve.wait_ge(s_sq, TT * b + t + 1)
                    V.tensor_reduce(ss[:, t, :], sq[:, t, :].rearrange("p (h d) -> p h d", d=HD), AX.X, ALU.add)\
                        .then_inc(s_ss, 1)
                dve.wait_ge(s_ss, TT * (b + 1))
                n = NEWTON * b
                V.tensor_scalar(ms[:, :, :], ss[:, :, :], 1.0 / HD, NORM_EPS, ALU.mult, ALU.add).then_inc(s_new, 1)
                dve.wait_ge(s_new, n + 1)
                V.tensor_scalar(nt[:, :, :].bitcast(i32), ms[:, :, :].bitcast(i32), 1, None, ALU.logical_shift_right)\
                    .then_inc(s_new, 1)
                dve.wait_ge(s_new, n + 2)
                V.tensor_scalar(rr[:, :, :].bitcast(i32), nt[:, :, :].bitcast(i32), -1.0, float(0x5F3759DF),
                                ALU.mult, ALU.add).then_inc(s_new, 1)
                for k in range(3):
                    dve.wait_ge(s_new, n + 3 * k + 3)
                    V.tensor_tensor(nt[:, :, :], rr[:, :, :], rr[:, :, :], ALU.mult).then_inc(s_new, 1)
                    dve.wait_ge(s_new, n + 3 * k + 4)
                    V.scalar_tensor_tensor(out=nt[:, :, :], in0=ms[:, :, :], scalar=-0.5, in1=nt[:, :, :],
                                           op0=ALU.mult, op1=ALU.mult).then_inc(s_new, 1)
                    dve.wait_ge(s_new, n + 3 * k + 5)
                    V.scalar_tensor_tensor(out=rr[:, :, :], in0=nt[:, :, :], scalar=1.5, in1=rr[:, :, :],
                                           op0=ALU.add, op1=ALU.mult).then_inc(s_new, 1)
                dve.wait_ge(s_new, n + NEWTON)
                for t in range(TT):
                    wait(dve, s_rope, TT * b)
                    V.tensor_tensor(qn[:, t, :].rearrange("p (h d) -> p h d", d=HD),
                                    bank[(1, 4)[t]][:, :].rearrange("p (h d) -> p h d", d=HD),
                                    rr[:, t, :].rearrange("p (h o) -> p h o", o=1).to_broadcast([P, 2 * H, HD]),
                                    ALU.mult).then_inc(s_qn, 1)

            def scale_w1():
                dve.wait_ge(s_wffn, 16 * N_FFN)
                for c in range(C):
                    for which, lo, hi in ((0, 0, LIGHT * P), (1, LIGHT * P, FCH * P)):
                        w = w1raw[:, c, lo:hi]
                        V.tensor_scalar(w, w, gam[:, which, c:c + 1], float(D) ** 0.5, ALU.mult, ALU.mult)\
                            .then_inc(s_scaled, 1)
                V.tensor_tensor(b2sum[:, :], b2[:, 0, :], b2[:, 1, :], ALU.add).then_inc(s_scaled, 1)
                dve.wait_ge(s_scaled, N_SCALED)
                V.tensor_copy(w1h[:, :, :], w1raw).then_inc(s_halved, 1)
                dve.wait_ge(s_halved, 1)
                V.tensor_tensor(w1l[:, :, :], w1raw, w1h[:, :, :].bitcast(f32), ALU.subtract).then_inc(s_w1, 1)

            def low_xn(b):
                dve.wait_ge(s_xnhigh, b + 1)
                wait(dve, s_h, FCH * b)
                V.tensor_tensor(xnl[:, :, :], bank[5][:, :].rearrange("p (c t) -> p c t", c=C),
                                xnh[:, :, :].bitcast(f32), ALU.subtract).then_inc(s_xnT, 1)

            def step(i):
                s, c, f, l = i, i - 1, i - 2, i - 3
                if first(c):
                    scale_w1()
                if live(s):
                    maxima(1, s, {NORM2_AT: lambda: normalise_heads(2, f)} if live(f) else {})
                elif live(f):
                    normalise_heads(2, f)
                if live(s):
                    max_t(1, s)
                if live(f):
                    dve.wait_ge(s_x1c, f + 1)
                    add_residual(2, f, PROJ_BANK, x1c)
                if live(f):
                    layer_norm(2, f)
                if live(c):
                    split(2, c, 1, 0)
                if live(f):
                    clamp2(f)
                if live(c):
                    split(2, c, 0, 1)
                if live(f):
                    scale2(f)
                if live(i + 1):
                    scaled_qk(i + 1)
                if starting(i + 1):
                    rotate(dve, V, i + 1)
                if live(f):
                    low_xn(f)
                if live(l):
                    dve.wait_ge(s_x2b, l + 1)
                    add_residual(3, l, FFN_BANK, x2b)
                if live(c):
                    maxima(2, c, {NORM1_AT: lambda: normalise_heads(1, s)} if live(s) else {})
                elif live(s):
                    normalise_heads(1, s)
                if live(s):
                    dve.wait_ge(s_x0, 16 * (s + 1))
                    add_residual(1, s, PROJ_BANK, x0)
                if live(c):
                    max_t(2, c)
                if live(i + 1):
                    split(1, i + 1, 0, 0)
                    split(1, i + 1, 1, 1)
                if first(i + 1):
                    more_rows()
                if live(s):
                    layer_norm(1, s)
                if live(l):
                    layer_norm(3, l)
            two_ones = float(np.array([0x3F803F80], np.uint32).view(np.float32)[0])

            def rows(a, s, lo, hi, value):
                V.memset(stk[a][s][lo:hi, :, :].bitcast(f32), value).then_inc(s_rows, 1)

            def more_rows():
                rows(2, 1, ROW_BIAS, K_ALL, two_ones)
                rows(2, 0, ROW_BIAS, ROW_BIAS + 1, two_ones)

            rows(1, 1, ROW_BIAS, K_ALL, two_ones)
            rows(1, 0, ROW_BIAS, ROW_BIAS + 1, two_ones)

            def halves(raw, parts, count):
                V.tensor_copy(parts[0][:, :, :], raw).then_inc(s_whalf, 1)
                dve.wait_ge(s_whalf, count + 1)
                V.tensor_tensor(parts[1][:, :, :], raw, parts[0][:, :, :].bitcast(f32), ALU.subtract).then_inc(s_whalf, 1)

            dve.wait_ge(s_wqk1, 16)
            halves(wqk1raw, wqk1, 0)
            dve.wait_ge(s_rows, 2)
            rows(1, 1, ROW_BIAS, ROW_BIAS + 1, 0.0)
            dve.wait_ge(s_kb, 16)
            V.tensor_copy(maskf[:, :], maski[:, :]).then_inc(s_mask, 1)
            dve.wait_ge(s_mask, 1)
            V.tensor_scalar(maskf[:, :], maskf[:, :], 0.0, None, ALU.is_equal).then_inc(s_mask, 1)
            dve.wait_ge(s_mask, 2)
            V.tensor_scalar(maskb[:, :], maskf[:, :], BIG, None, ALU.mult).then_inc(s_mask, 1)
            dve.wait_ge(s_wself, 16 * N_SELF)
            halves(wv1raw, wv1, 2)
            for t in range(TT):
                for s in range(2):
                    for half in range(2):
                        d = slice(half * h2, (half + 1) * h2)
                        V.tensor_tensor(ropeC[:, t, s, d], cs[:, t, 0, :], nw[:, s, d], ALU.mult).then_inc(s_table, 1)
                    V.scalar_tensor_tensor(out=ropeS[:, t, s, 0:h2], in0=cs[:, t, 1, :], scalar=-1.0,
                                           in1=nw[:, s, h2:HD], op0=ALU.mult, op1=ALU.mult).then_inc(s_table, 1)
                    V.tensor_tensor(ropeS[:, t, s, h2:HD], cs[:, t, 1, :], nw[:, s, 0:h2], ALU.mult).then_inc(s_table, 1)
            iterations(step, dve)

        @block.gpsimd
        def _(pool):
            G = nc.gpsimd

            def power(out, base, done, ready, b):
                pool.wait_ge(ready, b + 1)
                w = out.shape[-1]
                G.tensor_tensor(out, base, minus_half[:, 0:w], ALU.pow)\
                    .then_inc(done, 1)

            def mask_probs(a, b, between):
                for h in range(H):
                    if h in between:
                        between[h]()
                    wait_apart(pool, (s_exp[a], H * b + h + 1))
                    slot = pr[:, h % (2 * HG), :].rearrange("p (k t) -> p k t", t=P)[:, 0:3:2, :]
                    G.affine_select(out=slot, in_=slot, compare_op=ALU.is_ge, fill=0.0, base=0,
                                    pattern=[[0, 2], [1, P]], channel_multiplier=-1).then_inc(s_prob[a], 1)

            def step(i):
                s, c, f, l = i, i - 1, i - 2, i - 3
                if live(i + 1):
                    wait_apart(pool, (s_xhigh, i + 2), (s_v[1], i + 1))
                    G.tensor_tensor(xTp[1][:, :, :], xT[:, :, :], xTp[0][:, :, :].bitcast(f32), ALU.subtract)\
                        .then_inc(s_xlow, 1)
                if live(f):
                    power(rstd[2][:, :], ve[2][:, :], s_rs[2], s_ve[2], f)
                root = (lambda: power(rr2[:, :], ssm[:, :], s_sc2, s_ssm, f)) if live(f) else None
                if live(s):
                    mask_probs(1, s, {RR2_AT: root} if root else {})
                elif root:
                    root()
                if first(i):
                    pool.wait_ge(s_table, TT * 2 * 4)
                if live(i + 1) and not starting(i + 1):
                    rotate(pool, G, i + 1)
                if live(f):
                    if first(f):
                        pool.wait_ge(s_scaled, N_SCALED)
                    pool.wait_ge(s_x[2], TT * (f + 1))
                    wait(pool, s_y[3], f)
                    G.tensor_tensor(x2b[:, :, :], xo[2][:, :, :],
                                    b2sum[:, :].rearrange("p (o d) -> p o d", o=1).to_broadcast([P, TT, D]),
                                    ALU.add).then_inc(s_x2b, 1)
                if live(c):
                    wait_apart(pool, (s_x[1], TT * (c + 1)), (s_y[2], c))
                    G.tensor_copy(x1c[:, :, :], xo[1][:, :, :]).then_inc(s_x1c, 1)
                roots = {}
                if live(s):
                    roots[RSTD1_AT] = lambda: power(rstd[1][:, :], ve[1][:, :], s_rs[1], s_ve[1], s)
                if live(l):
                    roots[RSTD3_AT] = lambda: power(rstd[3][:, :], ve[3][:, :], s_rs[3], s_ve[3], l)
                if live(c):
                    mask_probs(2, c, roots)
                else:
                    for h in sorted(roots):
                        roots[h]()

            for m in (idf, idb):
                G.memset(m[:, :], 0.0).then_inc(s_pool, 1)
            G.memset(minus_half[:, :], -0.5)
            G.memset(cmaskb[:, :, :], 0.0)
            G.memset(cmask[:, :, :], 0.0).then_inc(s_pool, 1)
            for a in (1, 2):
                G.memset(va[a][:, :, :, :], 0.0).then_inc(s_pool, 1)
            pool.wait_ge(s_pool, 5)
            for m in (idf, idb):
                G.affine_select(out=m[:, :], in_=m[:, :], compare_op=ALU.not_equal, fill=1.0, base=0,
                                pattern=[[-1, P]], channel_multiplier=1)
            for diag, n in ((cmask[:, 1, :], 1), (cmaskb[:, :, :], 2)):
                G.affine_select(out=diag, in_=diag, compare_op=ALU.is_ge, fill=BIG, base=0,
                                pattern=[[0, 2], [-1, P]][2 - n:], channel_multiplier=1)
            for a in (1, 2):
                last = G.memset(va[a][:, :, :, HD:HD + 1], 1.0)
            last.then_inc(s_const, 1)
            iterations(step, pool)


MASKED_ON_PE = 1
VALUES_AFTER = 7
K2_AT = 6
OUT2_AT = (2, 3, 9, 14)
FFN_C = (3, 3, 6, 6, 8, 8, 12, 14, 15)
XN_AT = 10
HIDDEN_D = (1, 2, 4, 5, 7, 8, 10, 12, 14)
OUT1_AT = (1, 4, 8, 12)
FFN_F = (0, 0, 0, 0, 0, 3, 4, 6, 13)
V2_AT = 9
XNT_AT, COPY1_AT = 11, 4
NORM2_AT, NORM1_AT = 3, 4
RR2_AT, RSTD1_AT, RSTD3_AT = 0, 8, 12
NSTK = (None, 2 * len(TERMS_Q), 2 * len(TERMS_Q) + 1)
NEWTON = 3 + 3 * 3
N_SELF, N_CROSS, N_FFN = 3, 5, 8
N_SCALED = 2 * C + 1


def kernel(**inputs):
    import numpy as _np
    import concourse.bacc as _bacc
    from concourse import mybir as _mybir
    from concourse.bass_utils import run_bass_kernel_spmd as _run

    a = {k: _np.asarray(v) for k, v in inputs.items()}
    half = HD // 2
    freqs = _np.float32(32.0) ** (-_np.arange(0, HD, 2, dtype=_np.float32) / _np.float32(HD))
    angle = _np.arange(T, dtype=_np.float32)[:, None] * freqs[None, :].astype(_np.float32)

    def by_pairs(w):
        return w.reshape(D, HC, C, HD).transpose(0, 2, 3, 1).reshape(D, D)

    arrays = {
        "x": a["x"], "xT": a["x"].transpose(0, 2, 1), "ctxT": a["ctx_1024"].transpose(0, 2, 1),
        "mask": a["mask_BxS2_if1"],
        "wqk1": a["L0_attn_w_qkv"][:2 * D].T, "wv1": a["L0_attn_w_qkv"][2 * D:].T, "wo1": a["L0_attn_w_proj"].T,
        "wq2": by_pairs(a["L0_xattn_Wq"]), "wk2": by_pairs(a["L0_xattn_Wk"]), "wv2": a["L0_xattn_Wv"], "wo2": a["L0_xattn_Wo"],
        "w1h": a["L0_ffn_w1_h"].T, "w1l": a["L0_ffn_w1_l"].T, "w2h": a["L0_ffn_w2_h"].T, "w2l": a["L0_ffn_w2_l"].T,
        "b1h": a["L0_ffn_b1_h"].reshape(FCH - 1, P).T, "b1l": a["L0_ffn_b1_l"].reshape(1, P).T,
        "gam": _np.stack([a["L0_ffn_gamma_h"].reshape(C, P), a["L0_ffn_gamma_l"].reshape(C, P)]).transpose(2, 0, 1),
        "b2": _np.stack([a["L0_ffn_b2_h"], a["L0_ffn_b2_l"]]),
        "nw": _np.stack([a["L0_attn_q_norm_w"], a["L0_attn_k_norm_w"]]),
        "cossin": _np.concatenate([_np.cos(angle), _np.sin(angle)], axis=1).astype(_np.float32),
    }
    nc = _bacc.Bacc("TRN2", target_bir_lowering=False, num_devices=1)
    feed, io = {}, {}
    for name, value in arrays.items():
        value = _np.ascontiguousarray(value)
        feed[f"in_{name}"] = value
        io[name] = nc.dram_tensor(f"in_{name}", value.shape, _mybir.dt.from_np(value.dtype), kind="ExternalInput").ap()
    io["out"] = nc.dram_tensor("out_x", (B, T, D), _mybir.dt.float32, kind="ExternalOutput").ap()
    build(nc, io)
    r = _run(nc, [feed], core_ids=[0])
    return r.results[0]["out_x"]
```
